# Optimizing a Trainium2 kernel written in Bass

```python
import numpy as np
import jax
import jax.numpy as jnp

def _softmax(x, axis=-1):
    return jax.nn.softmax(x, axis=axis)

def _gelu(x):
    return jax.nn.gelu(x, approximate=True)

def _silu(x):
    return jax.nn.silu(x)

def _sigmoid(x):
    return jax.nn.sigmoid(x)

def _layernorm(x, axis=-1, eps=1e-05):
    m = jnp.mean(x, axis=axis, keepdims=True)
    v = jnp.var(x, axis=axis, keepdims=True)
    return (x - m) / jnp.sqrt(v + eps)

def _scatter_add(tgt, idx, src, axis=0):
    return tgt.at[idx].add(src)

def _segment_sum(src, seg, n):
    return jax.ops.segment_sum(src, seg, n)
kernel_name = 'mk_macaron_d1_jaxref_r8_21c69f'

def setup_inputs(seed: int=0):
    np.random.seed(seed)
    _w = jnp.asarray

    def _L0_attn_setup():
        import jax, jax.numpy as jnp
        import numpy as np
        HIDDEN = 256
        HEADS = 16
        HEAD_DIM = HIDDEN // HEADS
        key = jax.random.key(seed)
        kx, kq, kk, kv, ko = jax.random.split(key, 5)
        s = 1.0 / np.sqrt(HIDDEN)
        return {'x': jax.random.normal(kx, (2, 256, HIDDEN), dtype=jnp.float32), 'Wq': jax.random.normal(kq, (HIDDEN, HIDDEN), dtype=jnp.float32) * s, 'Wk': jax.random.normal(kk, (HIDDEN, HIDDEN), dtype=jnp.float32) * s, 'Wv': jax.random.normal(kv, (HIDDEN, HIDDEN), dtype=jnp.float32) * s, 'Wo': jax.random.normal(ko, (HIDDEN, HIDDEN), dtype=jnp.float32) * s}
    _L0_attn_in = _L0_attn_setup()

    def _L0_ffn_setup():
        import jax, jax.numpy as jnp
        import numpy as np
        HID = 256
        INTER = 1024
        NEXP = 8
        TOPK = 2
        EPS = 1e-05

        def _mock_fused_moe(x, selected_experts, routing_weights, expert_weight):
            y = jnp.einsum('bsh,hd->bsd', x, expert_weight)
            scale = routing_weights.sum(axis=-1, keepdims=True)
            return y * scale
        key = jax.random.key(seed)
        ks = jax.random.split(key, 6)
        s = lambda fan_in: 1.0 / np.sqrt(fan_in)
        return {'hidden_states': jax.random.normal(ks[0], (4, 512, HID), dtype=jnp.float32), 'gate_w': jax.random.uniform(ks[1], (HID, NEXP), jnp.float32, -s(HID), s(HID)), 'up_w': jax.random.uniform(ks[2], (HID, INTER), jnp.float32, -s(HID), s(HID)), 'down_w': jax.random.uniform(ks[3], (INTER, HID), jnp.float32, -s(INTER), s(INTER)), 'expert_weight': jax.random.normal(ks[4], (HID, HID), dtype=jnp.float32), 'ln_gamma': jnp.ones((HID,), jnp.float32), 'ln_beta': jnp.zeros((HID,), jnp.float32)}
    _L0_ffn_in = _L0_ffn_setup()
    _d = {'L0_attn_x': _L0_attn_in['x'], 'L0_attn_Wq': _L0_attn_in['Wq'], 'L0_attn_Wk': _L0_attn_in['Wk'], 'L0_attn_Wv': _L0_attn_in['Wv'], 'L0_attn_Wo': _L0_attn_in['Wo'], 'L0_ffn_gate_w': _L0_ffn_in['gate_w'], 'L0_ffn_up_w': _L0_ffn_in['up_w'], 'L0_ffn_down_w': _L0_ffn_in['down_w'], 'L0_ffn_expert_weight': _L0_ffn_in['expert_weight'], 'L0_ffn_ln_gamma': _L0_ffn_in['ln_gamma'], 'L0_ffn_ln_beta': _L0_ffn_in['ln_beta']}
    _x0 = _d['L0_attn_x']
    _d['L0_attn_x'] = jax.random.normal(jax.random.fold_in(jax.random.key(seed), 1), (1, 2048, 256), dtype=_x0.dtype)
    del _x0
    return _d

def reference(L0_attn_x, L0_attn_Wq, L0_attn_Wk, L0_attn_Wv, L0_attn_Wo, L0_ffn_gate_w, L0_ffn_up_w, L0_ffn_down_w, L0_ffn_expert_weight, L0_ffn_ln_gamma, L0_ffn_ln_beta):

    def _L0_attn_ref(x, Wq, Wk, Wv, Wo):
        import jax, jax.numpy as jnp
        import numpy as np
        HIDDEN = 256
        HEADS = 16
        HEAD_DIM = HIDDEN // HEADS
        b, s, _ = x.shape

        def split_heads(t):
            return t.reshape(b, s, HEADS, HEAD_DIM).transpose(0, 2, 1, 3)
        Q = split_heads(x @ Wq.T)
        K = split_heads(x @ Wk.T)
        V = split_heads(x @ Wv.T)
        scores = jnp.einsum('bhqd,bhkd->bhqk', Q, K) / jnp.sqrt(jnp.float32(HEAD_DIM))
        causal = jnp.tril(jnp.ones((s, s), dtype=bool))
        scores = jnp.where(causal, scores, jnp.float32(-jnp.inf))
        attn = jax.nn.softmax(scores, axis=-1)
        out = jnp.einsum('bhqk,bhkd->bhqd', attn, V)
        out = out.transpose(0, 2, 1, 3).reshape(b, s, HIDDEN)
        return out @ Wo.T

    def _L0_ffn_ref(hidden_states, gate_w, up_w, down_w, expert_weight, ln_gamma, ln_beta):
        import jax, jax.numpy as jnp
        import numpy as np
        HID = 256
        INTER = 1024
        NEXP = 8
        TOPK = 2
        EPS = 1e-05

        def _mock_fused_moe(x, selected_experts, routing_weights, expert_weight):
            y = jnp.einsum('bsh,hd->bsd', x, expert_weight)
            scale = routing_weights.sum(axis=-1, keepdims=True)
            return y * scale
        residuals = hidden_states
        logits = jnp.einsum('bsh,he->bse', hidden_states, gate_w)
        routing_weights, selected_experts = jax.lax.top_k(logits, TOPK)
        h = jnp.einsum('bsh,hi->bsi', residuals, up_w)
        h = jnp.square(jax.nn.relu(h))
        shared_out = jnp.einsum('bsi,ih->bsh', h, down_w)
        moe_out = _mock_fused_moe(hidden_states, selected_experts, routing_weights, expert_weight)
        y = shared_out + moe_out
        mu = y.mean(axis=-1, keepdims=True)
        var = jnp.mean(jnp.square(y - mu), axis=-1, keepdims=True)
        return (y - mu) * jax.lax.rsqrt(var + EPS) * ln_gamma + ln_beta
    x = L0_attn_x
    x = x + 0.5 * _L0_ffn_ref(_layernorm(x, axis=-1), L0_ffn_gate_w, L0_ffn_up_w, L0_ffn_down_w, L0_ffn_expert_weight, L0_ffn_ln_gamma, L0_ffn_ln_beta)
    x = x + _L0_attn_ref(_layernorm(x, axis=-1), L0_attn_Wq, L0_attn_Wk, L0_attn_Wv, L0_attn_Wo)
    x = x + 0.5 * _L0_ffn_ref(_layernorm(x, axis=-1), L0_ffn_gate_w, L0_ffn_up_w, L0_ffn_down_w, L0_ffn_expert_weight, L0_ffn_ln_gamma, L0_ffn_ln_beta)
    return x

_drawn_inputs = setup_inputs


def setup_inputs(seed=0):
    import zlib

    import numpy as np

    out = dict(_drawn_inputs(seed))
    spreads = {'L0_ffn_ln_gamma': (1.0, 0.2), 'L0_ffn_ln_beta': (0.0, 0.1)}
    factors = {}
    for name, (base, spread) in spreads.items():
        noise = np.random.default_rng([zlib.crc32(name.encode()), seed]).standard_normal(out[name].shape)
        drawn = base * np.exp(spread * noise) if base else spread * noise
        out[name] = jnp.asarray(drawn.astype(out[name].dtype))
    for name, factor in factors.items():
        out[name] = (out[name] * factor).astype(out[name].dtype)
    return out
```

```python
from contextlib import ExitStack

import concourse.bass as bass
from concourse import mybir

F32 = mybir.dt.float32
F32R = mybir.dt.float32r
BF16 = mybir.dt.bfloat16
ALU = mybir.AluOpType
ACT = mybir.ActivationFunctionType
AX = mybir.AxisListType

P = 128
S = 2048
D = 256
I = 1024
E = 8
H = 16
DH = D // H
KC = D // P
IC = I // P
CH = 512
NC = S // CH
TC = CH // P
NT = S // P
G = 4
NG = H // G
YW = D + E
PARTS = 6 * DH
NSH = 3
EPS = 1e-5
LOWEST = -3.0e38
SCALE = float(DH) ** -0.5
KB = 1024

UNITS = [(c, g) for c in range(NC) for g in range(NG)]
NU = len(UNITS)
STEPS = [(u, kt) for u, (c, g) in enumerate(UNITS) for kt in range(TC * c + TC)]
FIRST = [sum(TC * c + TC for c, _ in UNITS[:u]) for u in range(NU + 1)]
PIECES = [(u, i, ch, pair) for u, (c, g) in enumerate(UNITS) for i in range(TC) for ch in range(c + 1) for pair in range(2)]
LEAD = 4


def attention_plan():
    plan, done = [], [0]
    later = {}

    def at(step, *event):
        later.setdefault(min(step, len(STEPS) + 99), []).append(event)

    def pieces(until):
        while done[0] < min(until, len(PIECES)):
            u = PIECES[done[0]][0]
            plan.append(("max", done[0]))
            done[0] += 1
            for w in list(turning):
                turning[w] -= 1
                if not turning[w]:
                    plan.append(("turn", w))
                    del turning[w]
                    sending[w] = 5
            if done[0] == len(PIECES) or PIECES[done[0]][0] != u:
                plan.append(("top", u))
                turning[u] = 2

    turning, sending = {}, {}

    def tick(force=False):
        for w in list(turning):
            if done[0] == len(PIECES):
                plan.append(("turn", w))
                del turning[w]
                sending[w] = 5
        for w in list(sending):
            sending[w] -= 1
            if not sending[w] or force:
                plan.append(("rows", w))
                del sending[w]

    for u, (c, g) in enumerate(UNITS):
        at(FIRST[u + 1] + 3, "inv", u)
        at(FIRST[u + 1] + 6, "norm", u)
        if g == NG - 1:
            at(FIRST[u + 1] + 7, "proj", (c, 0))
            at(FIRST[u + 1] + 7, "proj", (c, 1))
    pieces(2 * (FIRST[1] + LEAD))
    tick(True)
    for s, (u, kt) in enumerate(STEPS):
        n = FIRST[u + 1] - FIRST[u]
        n_next = FIRST[u + 2] - FIRST[u + 1] if u + 2 <= NU else 0
        base = 2 * (FIRST[u + 1] + LEAD)
        k = s - FIRST[u]
        aim = [base + (2 * n_next * (4 * k + x)) // (4 * n) for x in (2, 4)]
        plan.append(("exp", (s, 0)))
        tick()
        plan.append(("exp", (s, 1)))
        tick()
        pieces(aim[0])
        plan.append(("exp", (s, 2)))
        tick()
        if s:
            plan.append(("pv", s - 1))
        plan.append(("exp", (s, 3)))
        tick()
        if s and STEPS[s - 1][0] != u:
            plan.append(("acc", u - 1))
        pieces(aim[1])
        plan.extend(later.pop(s, []))
    plan.append(("pv", len(STEPS) - 1))
    plan.append(("acc", NU - 1))
    for s in sorted(later):
        plan.extend(later[s])
    return plan


PLAN = attention_plan()


def slots_of(plan):
    uses = [e for e in plan if e[0] in ("max", "turn", "proj")]
    return {e: z for z, e in enumerate(uses)}


SLOT = slots_of(PLAN)
PROJECTED = [SLOT[("proj", (c, 1))] + 1 for c in range(NC)]
LAST_PIECE = [max(n for n, p in enumerate(PIECES) if p[0] == u) for u in range(NU)]


def build(nc, x_in, wqT, wkT, wvT, woT, gate_w, up_w, down_w, expert_w, gamma, beta, out):
    def at(name, kb, shape, dt):
        return nc.alloc_sbuf_tensor_at(name, shape, dt, offset=16512 + int(kb * KB))

    with ExitStack() as ctx:
        def sem(name):
            return ctx.enter_context(nc.semaphore(name))

        ident = at("ident", 0, [P, P], F32)
        mask = at("mask", 0.5, [P, P], F32)
        wo = at("wo", 1, [P, NG, D], F32)
        gam = at("gam", 5, [P, D], F32)
        bet = at("bet", 6, [P, D], F32)
        small = 7 * KB

        def tiny(name, shape, dt=F32):
            nonlocal small
            size = 4 if dt == F32 else 2
            for k in shape[1:]:
                size *= k
            t = at(name, small / KB, shape, dt)
            small += -(-size // 32) * 32
            return t

        eps_t = tiny("eps_t", [P, 1])
        stat = tiny("stat", [P, TC, 6])
        mv = tiny("mv", [P, TC, 2])
        sd = tiny("sd", [P, TC])
        rs = tiny("rs", [P, TC])
        stat2 = tiny("stat2", [P, 6])
        mv2 = tiny("mv2", [P, 2, 2])
        sd2 = tiny("sd2", [P, 2])
        rs2 = tiny("rs2", [P, 2])
        top8 = tiny("top8", [P, 8])
        route = tiny("route", [P, 2])
        assert small <= 8 * KB
        WU, WD, WG = KC * I, IC * D, KC * YW
        wall = at("wall", 8, [P, 2 * (WU + WD + WG)], F32R)
        wu = [wall[:, k * WU:(k + 1) * WU].rearrange("p (c n) -> p c n", c=KC) for k in range(2)]
        o = 2 * WU
        wd = [wall[:, o + k * WD:o + (k + 1) * WD].rearrange("p (c n) -> p c n", c=IC) for k in range(2)]
        o += 2 * WD
        wg = [wall[:, o + k * WG:o + (k + 1) * WG].rearrange("p (c n) -> p c n", c=KC) for k in range(2)]
        x = at("x", 45, [P, NT, D], F32)
        xn = at("xn", 61, [P, 2, TC, D], F32)
        xT = [[at(f"xT{b}{k}", 69 + 8 * b + 4 * k, [P, KC, CH], F32R) for k in range(2)] for b in range(2)]
        hT = [at(f"hT{k}", 85 + 16 * k, [P, IC, CH], F32R) for k in range(2)]
        relu = at("relu", 117, [P, 2, CH], F32)
        sq = at("sq", 121, [P, 2, CH], F32)
        moe = at("moe", 125, [P, 2, D], F32)
        y = at("y", 127, [P, 2, D], F32)
        yh = at("yh", 129, [P, 2, D], F32)
        raw_u = at("raw_u", 133, [P, KC, I], F32)
        raw_d = at("raw_d", 141, [P, IC, D], F32)
        raw_g = at("raw_g", 149, [P, KC, YW], F32)
        wp = [[at(f"wp{m}{k}", 154 + 4 * m + 2 * k, [P, KC, D], F32R) for k in range(2)] for m in range(3)]
        xq = at("xq", 166, [P, 2, TC, D], F32)
        xqn = at("xqn", 174, [P, TC, D], F32)
        xqT = [[at(f"xqT{b}{k}", 178 + 8 * b + 4 * k, [P, KC, CH], F32R) for k in range(2)] for b in range(2)]
        parts = at("parts", 194, [P, 2, 3, CH], BF16)
        rest = at("rest", 200, [P, 2, CH], F32)
        Q = at("Q", 8, [P, NC, H, CH], BF16)
        K = at("K", 72, [P, H, S], BF16)
        V = at("V", 136, [P, NT, H, DH + 1], F32)
        pr = at("pr", 154, [P, 3, G, CH], F32)
        att = at("att", 178, [P, NG, CH], F32)
        rb = at("rb", 186, [P, 2, CH], F32)
        x1t = at("x1t", 190, [P, TC, D], F32)
        mxp = at("mxp", 194, [P, 3, NC + 1, G, TC], F32)
        mcol = at("mcol", 195, [P, 2, G * TC], F32)
        mrow = at("mrow", 195.25, [G * TC, 2, NSH, P], BF16)
        mrest = at("mrest", 196.75, [G * TC, 2, P], F32)
        ones = at("ones", 197.75, [NSH, S], BF16)
        den = at("den", 201.75, [32, 2, 64], F32)
        inv = at("inv", 202.25, [32, 2, 64], F32)
        raw_w = at("raw_w", 194, [P, 3, KC, D], F32)

        ps = ctx.enter_context(nc.psum_tensor("ps", [P, 8, CH], F32))

        wall_d = nc.dram_tensor("wall_d", (P, 2 * (WU + WD + WG)), F32).ap()
        x1_d = nc.dram_tensor("x1_d", (S, D), F32).ap()
        x2_d = nc.dram_tensor("x2_d", (S, D), F32).ap()
        part_d = nc.dram_tensor("part_d", (2, 3, D, S), BF16).ap()
        den_d = nc.dram_tensor("den_d", (NU, G * CH), F32).ap()
        inv_d = nc.dram_tensor("inv_d", (NU, G * CH), F32).ap()

        def rows(ap, c):
            return ap[c * CH:(c + 1) * CH, :].rearrange("(t p) d -> p t d", p=P)

        x_loaded = [[sem(f"x_loaded{f}{c}") for c in range(NC)] for f in range(2)]
        wu_loaded, wd_loaded, wg_loaded, wp_loaded, wo_loaded, gb_loaded = (sem(n) for n in ("wu_loaded", "wd_loaded", "wg_loaded", "wp_loaded", "wo_loaded", "gb_loaded"))
        consts_ready = sem("consts_ready")
        w_hi, w_lo = sem("w_hi"), sem("w_lo")
        wall_stored, wall_back = sem("wall_stored"), sem("wall_back")
        gb_ready = sem("gb_ready")
        eps_ready = sem("eps_ready")
        dve = sem("dve")
        pool = sem("pool")
        mv_ready, sd_ready, xn_ready = sem("mv_ready"), sem("sd_ready"), sem("xn_ready")
        turned, xT_hi, xT_lo = sem("turned"), sem("xT_hi"), sem("xT_lo")
        up_done, relu_done, sq_done, hi_done, lo_done = (sem(n) for n in ("up_done", "relu_done", "sq_done", "hi_done", "lo_done"))
        moe_done, y_done = sem("moe_done"), sem("y_done")
        route_ready, moe_scaled, y_summed = sem("route_ready"), sem("moe_scaled"), sem("y_summed")
        mv2_ready, sd2_ready, yh_ready, x_done = (sem(n) for n in ("mv2_ready", "sd2_ready", "yh_ready", "x_done"))
        x1_stored = [sem(f"x1_stored{c}") for c in range(NC)]
        x2_stored = [sem(f"x2_stored{c}") for c in range(NC)]
        out_stored = sem("out_stored")
        xq_loaded = [sem(f"xq_loaded{c}") for c in range(NC)]
        pj_done, part_h, rest_done, part_m, part_l = (sem(n) for n in ("pj_done", "part_h", "rest_done", "part_m", "part_l"))
        vj_done, v_done, v_ones = sem("vj_done"), sem("v_done"), sem("v_ones")
        parts_stored = [sem(f"parts_stored{k}") for k in range(2)]
        qk_loaded = [sem(f"qk_loaded{c}") for c in range(NC)]
        ones_ready, ones_loaded = sem("ones_ready"), sem("ones_loaded")
        at_start = sem("at_start")
        slot_full, slot_free = sem("slot_full"), sem("slot_free")
        top_ready, mrow_ready = sem("top_ready"), sem("mrow_ready")
        m_loaded = [sem(f"m_loaded{k}") for k in range(2)]
        qk_done, exp_done, sel_done, pv_done, acc_out = (sem(n) for n in ("qk_done", "exp_done", "sel_done", "pv_done", "acc_out"))
        den_stored, den_loaded, inv_ready, inv_stored, norm_done = (sem(n) for n in ("den_stored", "den_loaded", "inv_ready", "inv_stored", "norm_done"))
        rb_loaded = [sem(f"rb_loaded{k}") for k in range(2)]
        x1t_loaded = sem("x1t_loaded")

        NF = NC
        FT = NC * TC
        TURN0 = 0

        def turn_no(phase, c):
            return phase * NC + c

        def diag_before(s):
            return sum(1 for u, kt in STEPS[:s] if kt >= TC * UNITS[u][0])

        DIAG = [diag_before(s) for s in range(len(STEPS) + 1)]
        block = ctx.enter_context(nc.Block())

        @block.sync
        def _(sp):
            sp.dma_start(x[:, 0:TC, :], rows(x_in, 0)).then_inc(x_loaded[0][0], 16)
            sp.dma_start(raw_u[:], up_w.rearrange("(c p) n -> p c n", p=P)).then_inc(wu_loaded, 16)
            sp.dma_start(raw_g[:, :, 0:D], expert_w.rearrange("(c p) n -> p c n", p=P)).then_inc(wg_loaded, 16)
            sp.dma_start(raw_g[:, :, D:YW], gate_w.rearrange("(c p) n -> p c n", p=P)).then_inc(wg_loaded, 16)
            sp.dma_start(raw_d[:], down_w.rearrange("(c p) n -> p c n", p=P)).then_inc(wd_loaded, 16)
            sp.dma_start(gam[:], gamma.rearrange("(a d) -> a d", a=1).broadcast_to([P, D])).then_inc(gb_loaded, 16)
            sp.dma_start(bet[:], beta.rearrange("(a d) -> a d", a=1).broadcast_to([P, D])).then_inc(gb_loaded, 16)
            for c in range(1, NC):
                sp.dma_start(x[:, TC * c:TC * c + TC, :], rows(x_in, c)).then_inc(x_loaded[0][c], 16)
            for m, w in enumerate((wqT, wkT, wvT)):
                sp.dma_start(raw_w[:, m], w.rearrange("(c p) n -> p c n", p=P)).then_inc(wp_loaded, 16)
            sp.dma_start(wo[:], woT.rearrange("g p n -> p g n")).then_inc(wo_loaded, 16)
            sp.wait_ge(w_hi, 3)
            sp.wait_ge(w_lo, 3)
            sp.dma_start(wall_d, wall[:].bitcast(F32)).then_inc(wall_stored, 16)
            for c in range(NC):
                sp.wait_ge(x_done, TC * (c + 1))
                sp.dma_start(rows(x1_d, c), x[:, TC * c:TC * c + TC, :]).then_inc(x1_stored[c], 16)
                sp.wait_ge(x1_stored[c], 16)
                if c < 2:
                    sp.dma_start(xq[:, c % 2], rows(x1_d, c)).then_inc(xq_loaded[c], 16)
            sp.wait_ge(wall_stored, 16)
            sp.wait_ge(y_summed, FT)
            for c in range(NC):
                if c + 2 < NC:
                    sp.wait_ge(xn_ready, turn_no(1, c) + 1)
                    sp.dma_start(xq[:, c % 2], rows(x1_d, c + 2)).then_inc(xq_loaded[c + 2], 16)
                for w in range(4):
                    n = 4 * c + w
                    m, hc = w // 2, w % 2
                    sp.wait_ge(part_l, n + 1)
                    sp.dma_start(part_d[m, :, hc * P:(hc + 1) * P, c * CH:(c + 1) * CH].rearrange("a d s -> d a s"),
                                 parts[:, n % 2]).then_inc(parts_stored[n % 2], 16)
                for k in range(2):
                    sp.wait_ge(parts_stored[k], 16 * (2 * c + 2))
                for r in range(6):
                    for m, dst, order in ((0, Q[:, c], (0, 0, 1, 1, 0, 2)), (1, K[:, :, c * CH:(c + 1) * CH], (0, 1, 0, 1, 2, 0))):
                        sp.dma_start(dst[r * DH:(r + 1) * DH],
                                     part_d[m, order[r], :, c * CH:(c + 1) * CH].rearrange("(h d) s -> d h s", d=DH)).then_inc(qk_loaded[c], 16)
            sp.wait_ge(ones_ready, 1)
            sp.dma_start(K[PARTS:PARTS + NSH], ones[:].rearrange("r (a s) -> r a s", a=1).broadcast_to([NSH, H, S])).then_inc(ones_loaded, 16)
            for u, (c, g) in enumerate(UNITS):
                if g == 0:
                    sp.wait_ge(vj_done, NT)
                    if c:
                        sp.wait_ge(x2_stored[c - 1], 16)
                    sp.dma_start(x1t[:], rows(x1_d, c)).then_inc(x1t_loaded, 16)
                sp.wait_ge(acc_out, u + 1)
                sp.dma_start(den_d[u].rearrange("(j q) -> j q", j=G), att[DH:P:32, g, :]).then_inc(den_stored, 16)
                sp.wait_ge(den_stored, 16 * (u + 1))
                if u >= 2:
                    sp.wait_ge(inv_ready, u - 1)
                sp.dma_start(den[:, u % 2], den_d[u].rearrange("(p q) -> p q", p=32)).then_inc(den_loaded, 16)
                sp.wait_ge(inv_ready, u + 1)
                sp.dma_start(inv_d[u].rearrange("(p q) -> p q", p=32), inv[:, u % 2]).then_inc(inv_stored, 16)
                sp.wait_ge(inv_stored, 16 * (u + 1))
                if u >= 2:
                    sp.wait_ge(norm_done, u - 1)
                sp.dma_start(rb[:, u % 2], inv_d[u].rearrange("(j a q) -> j a q", j=G, a=1).broadcast_to([G, 32, CH])).then_inc(rb_loaded[u % 2], 16)
                if u == 12:
                    sp.wait_ge(qk_done, 4 * FIRST[12])
                    sp.dma_start(wall[:].bitcast(F32), wall_d).then_inc(wall_back, 16)
                if g == NG - 1:
                    sp.wait_ge(slot_free, PROJECTED[c])
                    sp.dma_start(rows(x2_d, c), x1t[:]).then_inc(x2_stored[c], 16)
            sp.wait_ge(qk_done, 4 * len(STEPS))
            for c in range(NC):
                sp.wait_ge(x2_stored[c], 16)
                sp.dma_start(x[:, TC * c:TC * c + TC, :], rows(x2_d, c)).then_inc(x_loaded[1][c], 16)
            for c in range(NC):
                sp.wait_ge(x_done, FT + TC * (c + 1))
                sp.dma_start(rows(out, c), x[:, TC * c:TC * c + TC, :]).then_inc(out_stored, 16)
            sp.wait_ge(out_stored, 16 * NC)

        @block.gpsimd
        def _(gp):
            count = [0]

            def link(ins):
                count[0] += 1
                ins.then_inc(pool, 1)
                gp.wait_ge(pool, count[0])

            nc.gpsimd.memset(ident[:], 0.0).then_inc(consts_ready, 1)
            nc.gpsimd.memset(mask[:], 0.0).then_inc(consts_ready, 1)
            gp.wait_ge(consts_ready, 2)
            nc.gpsimd.affine_select(out=ident[:], in_=ident[:], compare_op=ALU.not_equal, fill=1.0, base=0,
                                    pattern=[[-1, P]], channel_multiplier=1).then_inc(consts_ready, 1)
            nc.gpsimd.affine_select(out=mask[:], in_=mask[:], compare_op=ALU.is_ge, fill=LOWEST, base=0,
                                    pattern=[[-1, P]], channel_multiplier=1).then_inc(consts_ready, 1)

            def ffn(f):
                for c in range(NC):
                    n = NF * f + c
                    for i in range(IC):
                        u = IC * n + i
                        gp.wait_ge(relu_done, u + 1)
                        if u >= 2:
                            gp.wait_ge(lo_done, u - 1)
                        nc.gpsimd.tensor_tensor(sq[:, u % 2], relu[:, u % 2], relu[:, u % 2], ALU.mult).then_inc(sq_done, 1)
                    for j in range(TC):
                        v = TC * n + j
                        gp.wait_ge(gb_ready, 2)
                        gp.wait_ge(yh_ready, v + 1)
                        link(nc.gpsimd.tensor_tensor(yh[:, v % 2], yh[:, v % 2], gam[:], ALU.mult))
                        link(nc.gpsimd.tensor_tensor(yh[:, v % 2], yh[:, v % 2], bet[:], ALU.add))
                        xt = x[:, TC * c + j]
                        nc.gpsimd.tensor_tensor(xt, xt, yh[:, v % 2], ALU.add).then_inc(x_done, 1)

            ffn(0)
            gp.wait_ge(y_done, FT)
            gp.wait_ge(w_lo, 3)
            gp.wait_ge(w_hi, 3)
            nc.gpsimd.memset(V[:, :, :, DH:DH + 1], 1.0).then_inc(v_ones, 1)
            for kind, what in PLAN:
                if kind == "exp" and what[1] == G - 1:
                    s = what[0]
                    u, kt = STEPS[s]
                    c = UNITS[u][0]
                    if kt >= TC * c:
                        q0 = P * (kt - TC * c)
                        gp.wait_ge(exp_done, G * (s + 1))
                        blk = pr[:, s % 3, :, q0:q0 + P]
                        nc.gpsimd.affine_select(out=blk, in_=blk, compare_op=ALU.is_ge, fill=0.0, base=0,
                                                pattern=[[0, G], [1, P]], channel_multiplier=-1).then_inc(sel_done, 1)
                elif kind == "norm":
                    g = UNITS[what][1]
                    gp.wait_ge(rb_loaded[what % 2], 16 * (what // 2 + 1))
                    gp.wait_ge(den_stored, 16 * (what + 1))
                    nc.gpsimd.tensor_tensor(att[:, g], att[:, g], rb[:, what % 2], ALU.mult).then_inc(norm_done, 1)
            ffn(1)

        @block.scalar
        def _(act):
            def weight_hi(dst, src, loaded, n):
                act.wait_ge(loaded, n)
                nc.scalar.copy(dst, src).then_inc(w_hi, 1)

            def sqrt_of(c_no):
                act.wait_ge(mv_ready, c_no + 1)
                nc.scalar.activation(sd[:], mv[:, :, 1], ACT.Sqrt, bias=eps_t[:, 0:1]).then_inc(sd_ready, 1)

            def turned_hi(c_no, dst):
                act.wait_ge(turned, c_no + 1)
                nc.scalar.copy(dst, ps[:, 0:KC, :]).then_inc(xT_hi, 1)

            def ffn(f):
                base = turn_no(2 * f, 0)
                sqrt_of(base)
                if f:
                    act.wait_ge(vj_done, NT)
                turned_hi(base, xT[0][0][:])
                for c in range(NC):
                    n = NF * f + c
                    if c + 1 < NC:
                        sqrt_of(base + c + 1)
                    for i in range(IC):
                        u = IC * n + i
                        act.wait_ge(up_done, u + 1)
                        if u >= 2:
                            act.wait_ge(sq_done, u - 1)
                        nc.scalar.activation(relu[:, u % 2], ps[:, 2 + u % 2, :], ACT.Relu).then_inc(relu_done, 1)
                        act.wait_ge(relu_done, u + 1)
                        if n and i == 0:
                            act.wait_ge(y_done, TC * n)
                        nc.scalar.activation(hT[0][:, i], relu[:, u % 2], ACT.Square).then_inc(hi_done, 1)
                    if c + 1 < NC:
                        if n >= 1:
                            act.wait_ge(y_done, TC * n)
                        turned_hi(base + c + 1, xT[(c + 1) % 2][0][:])
                    for j in range(TC):
                        v = TC * n + j
                        act.wait_ge(route_ready, v + 1)
                        if v >= 2:
                            act.wait_ge(y_summed, v - 1)
                        nc.scalar.mul(moe[:, v % 2], ps[:, 6 + v % 2, 0:D], route[:, v % 2:v % 2 + 1]).then_inc(moe_scaled, 1)
                        act.wait_ge(mv2_ready, v + 1)
                        nc.scalar.activation(sd2[:, v % 2:v % 2 + 1], mv2[:, v % 2, 1:2], ACT.Sqrt, bias=eps_t[:, 0:1]).then_inc(sd2_ready, 1)

            act.wait_ge(eps_ready, 1)
            weight_hi(wu[0], raw_u[:], wu_loaded, 16)
            weight_hi(wd[0], raw_d[:], wd_loaded, 16)
            weight_hi(wg[0], raw_g[:], wg_loaded, 32)
            for m in range(3):
                weight_hi(wp[m][0][:], raw_w[:, m], wp_loaded, 48)
            ffn(0)
            for c in range(NC):
                sqrt_of(turn_no(1, c))
                if c >= 2:
                    act.wait_ge(vj_done, TC * (c - 1))
                turned_hi(turn_no(1, c), xqT[c % 2][0][:])
                for w in range(4):
                    n = 4 * c + w
                    act.wait_ge(pj_done, n + 1)
                    if n >= 2:
                        act.wait_ge(parts_stored[n % 2], 16 * (n // 2))
                    if n == 0:
                        act.wait_ge(w_lo, 6)
                    nc.scalar.copy(parts[:, n % 2, 0], ps[:, 2 + n % 2, :]).then_inc(part_h, 1)
                    act.wait_ge(rest_done, n + 1)
                    nc.scalar.copy(parts[:, n % 2, 1], rest[:, n % 2]).then_inc(part_m, 1)
                for j in range(TC):
                    t = TC * c + j
                    act.wait_ge(vj_done, t + 1)
                    if t == 0:
                        act.wait_ge(v_ones, 1)
                    nc.scalar.copy(V[:, t, :, 0:DH], ps[:, 4 + t % 2, 0:D].rearrange("p (h d) -> p h d", h=H)).then_inc(v_done, 1)
            act.wait_ge(parts_stored[0], 16 * 2 * NC)
            act.wait_ge(parts_stored[1], 16 * 2 * NC)
            act.wait_ge(vj_done, NT)
            for kind, what in PLAN:
                if kind == "exp":
                    s, j = what
                    e = G * s + j
                    u, kt = STEPS[s]
                    c = UNITS[u][0]
                    q0 = max(0, P * (kt - TC * c))
                    act.wait_ge(qk_done, e + 1)
                    if s >= 3 and j == 0:
                        act.wait_ge(pv_done, s - 2)
                    nc.scalar.activation(pr[:, s % 3, j, q0:CH], ps[:, e % 3, q0:CH], ACT.Exp, scale=SCALE).then_inc(exp_done, 1)
                elif kind == "acc":
                    c, g = UNITS[what]
                    act.wait_ge(pv_done, FIRST[what + 1])
                    if c:
                        act.wait_ge(slot_full, PROJECTED[c - 1])
                    nc.scalar.copy(att[:, g], ps[:, 3, :]).then_inc(acc_out, 1)
                elif kind == "rows":
                    c, g = UNITS[what]
                    act.wait_ge(mrow_ready, what + 1)
                    if what == 0:
                        for k in range(1):
                            act.wait_ge(y_summed, FT)
                            act.wait_ge(wall_stored, 16)
                    for a in range(NSH):
                        act.dma_start(Q[PARTS + a:PARTS + a + 1, c, G * g:G * g + G, :].rearrange("o j (i q) -> o (j i) q", q=P),
                                      mrow[:, what % 2, a, :]).then_inc(m_loaded[what % 2], 16)
            ffn(1)

        @block.vector
        def _(v_):
            count = [0]

            def link(ins):
                count[0] += 1
                ins.then_inc(dve, 1)
                v_.wait_ge(dve, count[0])

            def weight_lo(dst, src, hi, n):
                v_.wait_ge(w_hi, n)
                nc.vector.tensor_tensor(dst, src, hi.bitcast(F32), ALU.subtract).then_inc(w_lo, 1)

            def layer_norm(c_no, src, dst, free_at):
                for j in range(TC):
                    last = nc.vector.bn_stats(stat[:, j], src[:, j])
                link(last)
                for j in range(TC):
                    last = nc.vector.bn_aggr(mv[:, j], stat[:, j])
                last.then_inc(mv_ready, 1)
                v_.wait_ge(sd_ready, c_no + 1)
                link(nc.vector.reciprocal(rs[:], sd[:]))
                if free_at:
                    v_.wait_ge(turned, free_at)
                for j in range(TC):
                    last = nc.vector.tensor_scalar(dst[:, j], src[:, j], mv[:, j, 0:1], rs[:, j:j + 1], ALU.subtract, ALU.mult)
                last.then_inc(xn_ready, 1)

            def turned_lo(c_no, dst, hi):
                v_.wait_ge(xT_hi, c_no + 1)
                nc.vector.tensor_tensor(dst, ps[:, 0:KC, :], hi.bitcast(F32), ALU.subtract).then_inc(xT_lo, 1)

            def ffn(f):
                base = turn_no(2 * f, 0)
                if f:
                    v_.wait_ge(qk_done, G * len(STEPS))
                    v_.wait_ge(pv_done, len(STEPS))
                    v_.wait_ge(norm_done, NU)
                v_.wait_ge(x_loaded[f][0], 16)
                layer_norm(base, x[:, 0:TC], xn[:, 0], 0)
                turned_lo(base, xT[0][1][:], xT[0][0][:])
                for c in range(NC):
                    n = NF * f + c
                    if c + 1 < NC:
                        v_.wait_ge(x_loaded[f][c + 1], 16)
                        layer_norm(base + c + 1, x[:, TC * (c + 1):TC * (c + 2)], xn[:, (c + 1) % 2], base + c if c else 0)
                    for i in range(IC):
                        u = IC * n + i
                        v_.wait_ge(hi_done, u + 1)
                        v_.wait_ge(sq_done, u + 1)
                        nc.vector.tensor_tensor(hT[1][:, i], sq[:, u % 2], hT[0][:, i].bitcast(F32), ALU.subtract).then_inc(lo_done, 1)
                    if c + 1 < NC:
                        turned_lo(base + c + 1, xT[(c + 1) % 2][1][:], xT[(c + 1) % 2][0][:])

                    def normalised(v):
                        k = v % 2
                        v_.wait_ge(sd2_ready, v + 1)
                        link(nc.vector.reciprocal(rs2[:, k:k + 1], sd2[:, k:k + 1]))
                        if v >= 2:
                            v_.wait_ge(x_done, v - 1)
                        nc.vector.tensor_scalar(yh[:, k], y[:, k], mv2[:, k, 0:1], rs2[:, k:k + 1], ALU.subtract, ALU.mult).then_inc(yh_ready, 1)

                    for j in range(TC):
                        v = TC * n + j
                        k = v % 2
                        v_.wait_ge(moe_done, v + 1)
                        link(nc.vector.max(top8[:], ps[:, 6 + k, D:YW]))
                        nc.vector.tensor_tensor(route[:, k:k + 1], top8[:, 0:1], top8[:, 1:2], ALU.add).then_inc(route_ready, 1)
                        if j:
                            normalised(v - 1)
                        v_.wait_ge(moe_scaled, v + 1)
                        v_.wait_ge(y_done, v + 1)
                        nc.vector.tensor_tensor(y[:, k], ps[:, 4 + k, 0:D], moe[:, k], ALU.add).then_inc(y_summed, 1)
                        v_.wait_ge(y_summed, v + 1)
                        link(nc.vector.bn_stats(stat2[:], y[:, k]))
                        nc.vector.bn_aggr(mv2[:, k], stat2[:]).then_inc(mv2_ready, 1)
                    normalised(TC * n + TC - 1)

            nc.vector.memset(eps_t[:], EPS).then_inc(eps_ready, 1)
            v_.wait_ge(wu_loaded, 16)
            weight_lo(wu[1], raw_u[:], wu[0], 1)
            weight_lo(wd[1], raw_d[:], wd[0], 2)
            weight_lo(wg[1], raw_g[:], wg[0], 3)
            for m in range(3):
                weight_lo(wp[m][1][:], raw_w[:, m], wp[m][0][:], 4 + m)
            v_.wait_ge(gb_loaded, 32)
            nc.vector.tensor_scalar(gam[:], gam[:], 0.5, None, ALU.mult).then_inc(gb_ready, 1)
            nc.vector.tensor_scalar(bet[:], bet[:], 0.5, None, ALU.mult).then_inc(gb_ready, 1)
            ffn(0)
            for c in range(NC):
                v_.wait_ge(xq_loaded[c], 16)
                layer_norm(turn_no(1, c), xq[:, c % 2], xqn[:], turn_no(1, c) if c else 0)
                turned_lo(turn_no(1, c), xqT[c % 2][1][:], xqT[c % 2][0][:])

                def low_part(n):
                    v_.wait_ge(part_m, n + 1)
                    nc.vector.tensor_tensor(parts[:, n % 2, 2], rest[:, n % 2], parts[:, n % 2, 1], ALU.subtract).then_inc(part_l, 1)

                for w in range(4):
                    n = 4 * c + w
                    v_.wait_ge(part_h, n + 1)
                    nc.vector.tensor_tensor(rest[:, n % 2], ps[:, 2 + n % 2, :], parts[:, n % 2, 0], ALU.subtract).then_inc(rest_done, 1)
                    if w:
                        low_part(n - 1)
                low_part(4 * c + 3)
            v_.wait_ge(parts_stored[0], 16 * 2 * NC)
            v_.wait_ge(parts_stored[1], 16 * 2 * NC)
            v_.wait_ge(part_l, 4 * NC)
            nc.vector.memset(ones[:], 1.0).then_inc(ones_ready, 1)
            nc.vector.memset(mxp[:], LOWEST).then_inc(at_start, 1)
            nc.vector.memset(ps[:, 3, :], 0.0).then_inc(at_start, 1)
            v_.wait_ge(at_start, 1)
            v_.wait_ge(consts_ready, 4)
            for event in PLAN:
                kind, what = event
                if kind == "max":
                    z = SLOT[event]
                    slot = ps[:, 4 + 2 * (z % 2):6 + 2 * (z % 2), :]
                    u, i, ch, pair = PIECES[what]
                    c = UNITS[u][0]
                    mx = mxp[:, u % 3]
                    v_.wait_ge(slot_full, z + 1)
                    if (i, ch, pair) == (0, 0, 0) and u >= 3:
                        v_.wait_ge(top_ready, u - 2)
                    off = CH if ch < c else P * i
                    if off:
                        last = nc.vector.tensor_reduce(mx[:, ch + 1, 2 * pair:2 * pair + 2, i], slot[:, :, 0:off], AX.X, ALU.max)
                    if ch == c:
                        for k in range(2):
                            blk = slot[:, k, P * i:P * i + P]
                            last = nc.vector.tensor_tensor_reduce(blk, blk, mask[:], 1.0, LOWEST, ALU.add, ALU.max,
                                                                  mx[:, 0, 2 * pair + k, i:i + 1])
                    last.then_inc(slot_free, 1)
                elif kind == "top":
                    c = UNITS[what][0]
                    v_.wait_ge(slot_free, SLOT[("max", LAST_PIECE[what])] + 1)
                    nc.vector.tensor_reduce(mcol[:, what % 2], mxp[:, what % 3, 0:c + 2].rearrange("p s j i -> p (j i) s"), AX.X,
                                            ALU.max).then_inc(top_ready, 1)
                elif kind == "turn":
                    z = SLOT[event]
                    b = what % 2
                    src = ps[0:G * TC, 4 + 2 * (z % 2), 0:P]
                    v_.wait_ge(slot_full, z + 1)
                    if what >= 2:
                        v_.wait_ge(m_loaded[b], 16 * NSH * (what // 2))
                    link(nc.vector.tensor_scalar(mrow[:, b, 0], src, -1.0, None, ALU.mult))
                    nc.vector.scalar_tensor_tensor(out=mrest[:, b], in0=src, scalar=-1.0, in1=mrow[:, b, 0],
                                                   op0=ALU.mult, op1=ALU.subtract).then_inc(slot_free, 1)
                    v_.wait_ge(slot_free, z + 1)
                    link(nc.vector.tensor_copy(mrow[:, b, 1], mrest[:, b]))
                    nc.vector.tensor_tensor(mrow[:, b, 2], mrest[:, b], mrow[:, b, 1], ALU.subtract).then_inc(mrow_ready, 1)
                elif kind == "inv":
                    v_.wait_ge(den_loaded, 16 * (what + 1))
                    if what >= 2:
                        v_.wait_ge(inv_stored, 16 * (what - 1))
                    nc.vector.reciprocal(inv[:, what % 2], den[:, what % 2]).then_inc(inv_ready, 1)
                elif kind == "proj":
                    c, half = what
                    z = SLOT[event]
                    v_.wait_ge(slot_full, z + 1)
                    v_.wait_ge(x1t_loaded, 16 * (c + 1))
                    xt = x1t[:, 2 * half:2 * half + 2, :]
                    nc.vector.tensor_tensor(xt, ps[:, 4 + 2 * (z % 2):6 + 2 * (z % 2), 0:D], xt, ALU.add).then_inc(slot_free, 1)
            ffn(1)

        @block.tensor
        def _(pe):
            def turn(c_no, src, free):
                pe.wait_ge(xn_ready, c_no + 1)
                if c_no:
                    pe.wait_ge(xT_hi, c_no)
                    pe.wait_ge(xT_lo, c_no)
                for j in range(TC):
                    for k in range(KC):
                        mm = nc.tensor.transpose(ps[:, k, P * j:P * j + P], src[:, j, P * k:P * k + P], ident[:])
                mm.then_inc(turned, 1)

            def product(dst, lhs, rhs, chunks):
                n = 0
                for k in chunks:
                    for a, b in ((0, 0), (0, 1), (1, 0)):
                        mm = nc.tensor.matmul(dst, lhs(a, k), rhs(b, k), start=(n == 0), stop=(n == 3 * len(chunks) - 1))
                        n += 1
                return mm

            def ffn(f):
                base = turn_no(2 * f, 0)
                if f:
                    pe.wait_ge(slot_free, PROJECTED[NC - 1])
                    pe.wait_ge(wall_back, 16)
                turn(base, xn[:, 0], 0)
                pe.wait_ge(w_hi, 1)
                pe.wait_ge(w_lo, 1)
                for c in range(NC):
                    n = NF * f + c
                    xt = xT[c % 2]
                    pe.wait_ge(xT_hi, base + c + 1)
                    pe.wait_ge(xT_lo, base + c + 1)
                    for i in range(IC):
                        u = IC * n + i
                        if u >= 2:
                            pe.wait_ge(relu_done, u - 1)
                        product(ps[:, 2 + u % 2, :], lambda a, k: wu[a][:, k, P * i:P * i + P], lambda b, k: xt[b][:, k, :],
                                range(KC)).then_inc(up_done, 1)
                    if c + 1 < NC:
                        turn(base + c + 1, xn[:, (c + 1) % 2], 0)
                    if n == 0:
                        pe.wait_ge(w_hi, 3)
                        pe.wait_ge(w_lo, 3)
                    for j in range(TC):
                        v = TC * n + j
                        if v >= 2:
                            pe.wait_ge(moe_scaled, v - 1)
                            pe.wait_ge(y_summed, v - 1)
                            pe.wait_ge(route_ready, v - 1)
                        product(ps[:, 6 + v % 2, 0:YW], lambda a, k: xt[a][:, k, P * j:P * j + P], lambda b, k: wg[b][:, k, :],
                                range(KC)).then_inc(moe_done, 1)
                        for i in range(IC):
                            if j == 0:
                                pe.wait_ge(lo_done, IC * n + i + 1)
                            for m, (a, b) in enumerate(((0, 0), (0, 1), (1, 0))):
                                mm = nc.tensor.matmul(ps[:, 4 + v % 2, 0:D], hT[a][:, i, P * j:P * j + P], wd[b][:, i, :],
                                                      start=(i == 0 and m == 0), stop=(i == IC - 1 and m == 2))
                        mm.then_inc(y_done, 1)

            pe.wait_ge(consts_ready, 4)
            ffn(0)
            pe.wait_ge(w_hi, 6)
            pe.wait_ge(w_lo, 6)
            for c in range(NC):
                c_no = turn_no(1, c)
                turn(c_no, xqn, 0)
                if c == 0:
                    pe.wait_ge(relu_done, IC * NF)
                    pe.wait_ge(y_summed, FT)
                pe.wait_ge(xT_hi, c_no + 1)
                pe.wait_ge(xT_lo, c_no + 1)
                xt = xqT[c % 2]
                for w in range(4):
                    n = 4 * c + w
                    m, hc = w // 2, w % 2
                    if n >= 2:
                        pe.wait_ge(rest_done, n - 1)
                    product(ps[:, 2 + n % 2, :], lambda a, k: wp[m][a][:, k, P * hc:P * hc + P], lambda b, k: xt[b][:, k, :],
                            range(KC)).then_inc(pj_done, 1)
                for j in range(TC):
                    t = TC * c + j
                    if t >= 2:
                        pe.wait_ge(v_done, t - 1)
                    product(ps[:, 4 + t % 2, 0:D], lambda a, k: xt[a][:, k, P * j:P * j + P], lambda b, k: wp[2][b][:, k, :],
                            range(KC)).then_inc(vj_done, 1)
            pe.wait_ge(v_done, NT)
            pe.wait_ge(part_l, 4 * NC)
            pe.wait_ge(at_start, 2)
            pe.wait_ge(ones_loaded, 16)
            pe.wait_ge(wo_loaded, 16)
            for event in PLAN:
                kind, what = event
                if kind == "max":
                    z = SLOT[event]
                    u, i, ch, pair = PIECES[what]
                    c, g = UNITS[u]
                    if z >= 2:
                        pe.wait_ge(slot_free, z - 1)
                    if (g, i, ch, pair) == (0, 0, 0, 0):
                        pe.wait_ge(qk_loaded[c], 16 * 12)
                    w = CH if ch < c else P * (i + 1)
                    for k in range(2):
                        h = G * g + 2 * pair + k
                        mm = nc.tensor.matmul(ps[:, 4 + 2 * (z % 2) + k, 0:w], Q[0:PARTS, c, h, P * i:P * i + P],
                                              K[0:PARTS, h, CH * ch:CH * ch + w], start=True, stop=True)
                    mm.then_inc(slot_full, 1)
                elif kind == "turn":
                    z = SLOT[event]
                    pe.wait_ge(slot_free, z - 1)
                    pe.wait_ge(top_ready, what + 1)
                    nc.tensor.transpose(ps[0:G * TC, 4 + 2 * (z % 2), 0:P], mcol[:, what % 2], ident[:]).then_inc(slot_full, 1)
                elif kind == "exp":
                    s, j = what
                    e = G * s + j
                    u, kt = STEPS[s]
                    c, g = UNITS[u]
                    if e >= 3:
                        pe.wait_ge(exp_done, e - 2)
                    if kt == 0 and j == 0:
                        pe.wait_ge(m_loaded[u % 2], 16 * NSH * (u // 2 + 1))
                    q0 = max(0, P * (kt - TC * c))
                    h = G * g + j
                    nc.tensor.matmul(ps[:, e % 3, q0:CH], K[0:PARTS + NSH, h, P * kt:P * kt + P], Q[0:PARTS + NSH, c, h, q0:CH],
                                     start=True, stop=True).then_inc(qk_done, 1)
                elif kind == "pv":
                    s = what
                    u, kt = STEPS[s]
                    c, g = UNITS[u]
                    q0 = max(0, P * (kt - TC * c))
                    pe.wait_ge(exp_done, G * (s + 1))
                    if kt >= TC * c:
                        pe.wait_ge(sel_done, DIAG[s + 1])
                    if kt == 0 and u:
                        pe.wait_ge(acc_out, u)
                    for j in range(G):
                        mm = nc.tensor.matmul(ps[32 * j:32 * j + DH + 1, 3, q0:CH], V[:, kt, G * g + j, :], pr[:, s % 3, j, q0:CH],
                                              start=(kt == 0), stop=(kt == TC * c + TC - 1))
                    mm.then_inc(pv_done, 1)
                elif kind == "proj":
                    c, half = what
                    z = SLOT[event]
                    pe.wait_ge(slot_free, z - 1)
                    pe.wait_ge(norm_done, NG * (c + 1))
                    for k in range(2):
                        t = 2 * half + k
                        for g in range(NG):
                            mm = nc.tensor.matmul(ps[:, 4 + 2 * (z % 2) + k, 0:D], att[:, g, P * t:P * t + P], wo[:, g, :],
                                                  start=(g == 0), stop=(g == NG - 1))
                    mm.then_inc(slot_full, 1)
            ffn(1)


def kernel(L0_attn_x, L0_attn_Wq, L0_attn_Wk, L0_attn_Wv, L0_attn_Wo, L0_ffn_gate_w, L0_ffn_up_w, L0_ffn_down_w,
           L0_ffn_expert_weight, L0_ffn_ln_gamma, L0_ffn_ln_beta):
    import numpy as np
    import concourse.bacc as bacc
    from concourse.bass_utils import run_bass_kernel_spmd

    wo = np.asarray(L0_attn_Wo)
    woT = np.zeros((NG, G, 32, D), wo.dtype)
    woT[:, :, :DH, :] = wo.T.reshape(NG, G, DH, D)
    arrays = {
        "x": np.asarray(L0_attn_x).reshape(S, D),
        "wqT": np.ascontiguousarray(np.asarray(L0_attn_Wq).T),
        "wkT": np.ascontiguousarray(np.asarray(L0_attn_Wk).T),
        "wvT": np.ascontiguousarray(np.asarray(L0_attn_Wv).T),
        "woT": woT.reshape(NG, P, D),
        "gate_w": np.ascontiguousarray(L0_ffn_gate_w),
        "up_w": np.ascontiguousarray(L0_ffn_up_w),
        "down_w": np.ascontiguousarray(L0_ffn_down_w),
        "expert_w": np.ascontiguousarray(L0_ffn_expert_weight),
        "gamma": np.ascontiguousarray(L0_ffn_ln_gamma),
        "beta": np.ascontiguousarray(L0_ffn_ln_beta),
    }
    nc = bacc.Bacc("TRN2", target_bir_lowering=False, num_devices=1)
    args = [nc.dram_tensor(f"in_{n}", a.shape, mybir.dt.from_np(a.dtype), kind="ExternalInput").ap() for n, a in arrays.items()]
    res = nc.dram_tensor("res", (S, D), F32, kind="ExternalOutput").ap()
    build(nc, *args, res)
    r = run_bass_kernel_spmd(nc, [{f"in_{n}": a for n, a in arrays.items()}], core_ids=[0])
    return r.results[0]["res"].reshape(1, S, D)
```

```python
from contextlib import ExitStack

import concourse.bass as bass
from concourse import mybir

F32 = mybir.dt.float32
F32R = mybir.dt.float32r
BF16 = mybir.dt.bfloat16
ALU = mybir.AluOpType
ACT = mybir.ActivationFunctionType
AX = mybir.AxisListType

P = 128
S = 2048
D = 256
I = 1024
E = 8
H = 16
DH = D // H
KC = D // P
IC = I // P
CH = 512
NC = S // CH
TC = CH // P
NT = S // P
IH = I // 2
G = 4
NG = H // G
YW = D + E
PARTS = 6 * DH
NSH = 3
EPS = 1e-5
LOWEST = -3.0e38
SCALE = float(DH) ** -0.5
KB = 1024
PJ = (2, 3, 6, 7)
NB = 4

UNITS = [(c, g) for c in range(NC) for g in range(NG)]
NU = len(UNITS)
STEPS = [(u, kt) for u, (c, g) in enumerate(UNITS) for kt in range(TC * c + TC)]
FIRST = [sum(TC * c + TC for c, _ in UNITS[:u]) for u in range(NU + 1)]
PIECES = [(u, i, ch, pair) for u, (c, g) in enumerate(UNITS) for i in range(TC) for ch in range(c + 1) for pair in range(2)]
NR = 2
LAG = 2
LEAD = 5
STATS_AT = 2
TURN_AFTER = 1
LAST_PROJ = 3


def attention_plan():
    plan, done = [], [0]
    later, turning, sending = {}, {}, {}

    def width(s):
        u, kt = STEPS[s]
        return CH - max(0, P * (kt - TC * UNITS[u][0]))

    step_cost = [G * (2 * width(s) + 60) for s in range(len(STEPS))]
    piece_cost = []
    for u, i, ch, pair in PIECES:
        piece_cost.append(2 * CH + 60 if ch < UNITS[u][0] else 2 * P * (i + 1) + 300)

    def at(step, *event):
        later.setdefault(step, []).append(event)

    def turns():
        for w in list(turning):
            turning[w] -= 1
            if turning[w] <= 0 or done[0] == len(PIECES):
                plan.append(("turn", w))
                del turning[w]
                sending[w] = 5

    def piece():
        u = PIECES[done[0]][0]
        plan.append(("max", done[0]))
        done[0] += 1
        turns()
        if done[0] == len(PIECES) or PIECES[done[0]][0] != u:
            plan.append(("top", u))
            turning[u] = 2

    def tick(force=False):
        if done[0] == len(PIECES):
            turns()
        for w in list(sending):
            sending[w] -= 1
            if not sending[w] or force:
                plan.append(("rows", w))
                del sending[w]

    for u, (c, g) in enumerate(UNITS):
        at(FIRST[u + 1] + LAG + 2, "inv", u)
        at(FIRST[u + 1] + LAG + 5, "norm", u)
        if g == NG - 1 and c < NC - 1:
            at(FIRST[u + 1] + LAG + 5, "proj", (c, 0))
            at(FIRST[u + 1] + LAG + 6, "proj", (c, 1))
    while done[0] < 2 * (FIRST[1] + LEAD):
        piece()
    tick(True)
    for s, (u, kt) in enumerate(STEPS):
        start, end = FIRST[u], FIRST[u + 1]
        if kt == 0:
            goal = min(len(PIECES), 2 * (FIRST[min(u + 2, NU)] + LEAD)) if u + 1 < NU else len(PIECES)
            ahead = sum(piece_cost[done[0]:goal])
            total = sum(step_cost[start:end - (LEAD if u == NU - 2 else 0)])
            spent = 0
            given = 0
        for j in range(G):
            plan.append(("exp", (s, j)))
            tick()
            if j == 2 and s >= LAG:
                plan.append(("pv", s - LAG))
                if STEPS[s - LAG + 1][0] != STEPS[s - LAG][0]:
                    acc = STEPS[s - LAG][0]
            spent += step_cost[s] / G
            if j == 3 and s >= LAG and STEPS[s - LAG + 1][0] != STEPS[s - LAG][0]:
                plan.append(("acc", STEPS[s - LAG][0]))
            while done[0] < goal and given + piece_cost[done[0]] / 2 <= ahead * spent / total:
                given += piece_cost[done[0]]
                piece()
        if s == end - 1:
            while done[0] < goal:
                piece()
        plan.extend(later.pop(s, []))
        if s == FIRST[NU - 2]:
            plan.append(("norm_x", None))
    for s in range(len(STEPS) - LAG, len(STEPS)):
        plan.append(("pv", s))
    plan.append(("acc", NU - 1))
    for s in sorted(later):
        plan.extend(later[s])
    return plan


PLAN = attention_plan()


def slots_of(plan):
    uses = [e for e in plan if e[0] in ("max", "turn", "proj")]
    return {e: z for z, e in enumerate(uses)}


SLOT = slots_of(PLAN)
PROJECTED = [SLOT[("proj", (c, 1))] + 1 for c in range(NC - 1)]
SLOTS = len(SLOT)
LAST_PIECE = [max(n for n, p in enumerate(PIECES) if p[0] == u) for u in range(NU)]


def build(nc, x_in, wqT, wkT, wvT, woT, gate_w, up_w, down_w, expert_w, gamma, beta, out):
    def at(name, kb, shape, dt):
        return nc.alloc_sbuf_tensor_at(name, shape, dt, offset=16512 + int(kb * KB))

    with ExitStack() as ctx:
        def sem(name):
            return ctx.enter_context(nc.semaphore(name))

        ident = at("ident", 0, [P, P], F32)
        mask = at("mask", 0.5, [P, P], F32)
        wo = at("wo", 1, [P, NG, D], F32)
        gam = at("gam", 5, [P, D], F32)
        bet = at("bet", 6, [P, D], F32)
        small = 7 * KB

        def tiny(name, shape, dt=F32):
            nonlocal small
            size = 4 if dt == F32 else 2
            for k in shape[1:]:
                size *= k
            t = at(name, small / KB, shape, dt)
            small += -(-size // 32) * 32
            return t

        eps_t = tiny("eps_t", [P, 1])
        stat = tiny("stat", [P, TC, 6])
        mv = tiny("mv", [P, TC, 2])
        sd = tiny("sd", [P, TC])
        rs = tiny("rs", [P, TC])
        stat2 = tiny("stat2", [P, 6])
        mv2 = tiny("mv2", [P, 2, 2])
        sd2 = tiny("sd2", [P, 2])
        rs2 = tiny("rs2", [P, 2])
        top8 = tiny("top8", [P, 8])
        route = tiny("route", [P, 2])
        assert small <= 8 * KB
        WU, WD, WG = KC * I, IC * D, KC * YW
        wall = at("wall", 8, [P, 2 * (WU + WD + WG)], F32R)
        wu = [wall[:, k * WU:(k + 1) * WU].rearrange("p (c n) -> p c n", c=KC) for k in range(2)]
        o = 2 * WU
        wd = [wall[:, o + k * WD:o + (k + 1) * WD].rearrange("p (c n) -> p c n", c=IC) for k in range(2)]
        o += 2 * WD
        wg = [wall[:, o + k * WG:o + (k + 1) * WG].rearrange("p (c n) -> p c n", c=KC) for k in range(2)]
        x = at("x", 52.125, [P, NT, D], F32)
        xn = at("xn", 44.125, [P, 2, TC, D], F32)
        xT = [[at(f"xT{b}{k}", 68.5 + 8 * b + 4 * k, [P, KC, CH], F32R) for k in range(2)] for b in range(2)]
        hT = [at(f"hT{k}", 85 + 16 * k, [P, IC, CH], F32R) for k in range(2)]
        relu = at("relu", 117, [P, NR, CH], F32)
        sq = at("sq", 121, [P, 2, CH], F32)
        moe = at("moe", 125, [P, 2, D], F32)
        y = at("y", 127, [P, 2, D], F32)
        yh = at("yh", 129, [P, 2, D], F32)
        raw_u = at("raw_u", 133, [P, KC, I], F32)
        raw_d = at("raw_d", 141, [P, IC, D], F32)
        raw_g = at("raw_g", 149, [P, KC, YW], F32)
        wp = [[at(f"wp{m}{k}", 154 + 4 * m + 2 * k, [P, KC, D], F32R) for k in range(2)] for m in range(3)]
        xqT = [[at(f"xqT{b}{k}", 178 + 8 * b + 4 * k, [P, KC, CH], F32R) for k in range(2)] for b in range(2)]
        parts = at("parts", 166, [P, NB, 3, CH], BF16)
        rest = at("rest", 194, [P, 2, CH], F32)
        NRE = 2
        Q = at("Q", 8.125, [P, NC, H, CH], BF16)
        K = at("K", 72.125, [P, H, S], BF16)
        V = at("V", 136.125, [P, NT, H, DH + 1], F32)
        pr = at("pr", 154, [P, 3, G, CH], F32)
        att = at("att", 178, [P, NG, CH], F32)
        rb = at("rb", 186, [P, 2, CH], F32)
        x1t = at("x1t", 190, [P, TC, D], F32)
        mrow = at("mrow", 194, [G * TC, 2, NSH, P], BF16)
        mrest = at("mrest", 195.5, [G * TC, 2, P], F32)
        den = at("den", 196.5, [32, 2, 64], F32)
        inv = at("inv", 197, [32, 2, 64], F32)
        raw_w = at("raw_w", 198, [P, 3, KC, D], F32)
        mxp = at("mxp", 204, [P, 3, NC + 1, G, TC], F32)
        mcol = at("mcol", 205, [P, 2, G * TC], F32)
        ones = at("ones", 205.25, [NSH, CH], BF16)

        ps = ctx.enter_context(nc.psum_tensor("ps", [P, 8, CH], F32))

        wall_d = nc.dram_tensor("wall_d", (P, 2 * (WU + WD + WG)), F32).ap()
        x1_d = nc.dram_tensor("x1_d", (S, D), F32).ap()
        x2_d = nc.dram_tensor("x2_d", (S, D), F32).ap()
        part_d = nc.dram_tensor("part_d", (2, 3, D, S), BF16).ap()
        den_d = nc.dram_tensor("den_d", (NU, G * CH), F32).ap()
        inv_d = nc.dram_tensor("inv_d", (NU, G * CH), F32).ap()

        def rows(ap, c):
            return ap[c * CH:(c + 1) * CH, :].rearrange("(t p) d -> p t d", p=P)

        x_loaded = [[sem(f"x_loaded{f}{c}") for c in range(NC)] for f in range(2)]
        wu_loaded, wv_loaded, wd_loaded, wg_loaded, wp_loaded, wo_loaded, gb_loaded = (sem(n) for n in ("wu_loaded", "wv_loaded", "wd_loaded", "wg_loaded", "wp_loaded", "wo_loaded", "gb_loaded"))
        consts_ready = sem("consts_ready")
        w_hi, w_lo = sem("w_hi"), sem("w_lo")
        wall_stored, wall_back = sem("wall_stored"), sem("wall_back")
        gb_ready = sem("gb_ready")
        eps_ready = sem("eps_ready")
        dve = sem("dve")
        pool = sem("pool")
        stats_done, mv_ready, sd_ready, xn_ready = sem("stats_done"), sem("mv_ready"), sem("sd_ready"), sem("xn_ready")
        turned, xT_hi, xT_lo = sem("turned"), sem("xT_hi"), sem("xT_lo")
        up_done, relu_done, sq_done, hi_done, lo_done = (sem(n) for n in ("up_done", "relu_done", "sq_done", "hi_done", "lo_done"))
        moe_done, y_done = sem("moe_done"), sem("y_done")
        route_ready, moe_scaled, y_summed = sem("route_ready"), sem("moe_scaled"), sem("y_summed")
        mv2_ready, sd2_ready, yh_ready, x_beta, x_done = (sem(n) for n in ("mv2_ready", "sd2_ready", "yh_ready", "x_beta", "x_done"))
        x1_stored = [sem(f"x1_stored{c}") for c in range(NC)]
        x2_stored = [sem(f"x2_stored{c}") for c in range(NC)]
        out_stored = sem("out_stored")
        pj_done, part_h, rest_done, part_m, part_l = (sem(n) for n in ("pj_done", "part_h", "rest_done", "part_m", "part_l"))
        vj_done, v_done, v_ones = sem("vj_done"), sem("v_done"), sem("v_ones")
        parts_stored = [sem(f"parts_stored{k}") for k in range(NB)]
        qk_loaded = [sem(f"qk_loaded{c}") for c in range(NC)]
        ones_ready, ones_loaded = sem("ones_ready"), sem("ones_loaded")
        at_start = sem("at_start")
        slot_full, slot_free = sem("slot_full"), sem("slot_free")
        top_ready, mrow_ready = sem("top_ready"), sem("mrow_ready")
        m_loaded = [sem(f"m_loaded{k}") for k in range(2)]
        qk_done, exp_done, sel_done, pv_done, acc_out = (sem(n) for n in ("qk_done", "exp_done", "sel_done", "pv_done", "acc_out"))
        den_stored, den_loaded, inv_ready, inv_stored, norm_done = (sem(n) for n in ("den_stored", "den_loaded", "inv_ready", "inv_stored", "norm_done"))
        rb_loaded = [sem(f"rb_loaded{k}") for k in range(2)]
        x1t_loaded = sem("x1t_loaded")

        NF = NC
        FT = NC * TC

        def turn_no(phase, c):
            return phase * NC + c

        def diag_before(s):
            return sum(1 for u, kt in STEPS[:s] if kt >= TC * UNITS[u][0])

        DIAG = [diag_before(s) for s in range(len(STEPS) + 1)]
        block = ctx.enter_context(nc.Block())

        @block.sync
        def _(sp):
            sp.dma_start(x[:, 0:TC, :], rows(x_in, 0)).then_inc(x_loaded[0][0], 16)
            for k, loaded in enumerate((wu_loaded, wv_loaded)):
                sp.dma_start(raw_u[:, :, k * IH:(k + 1) * IH], up_w.rearrange("(c p) n -> p c n", p=P)[:, :, k * IH:(k + 1) * IH]).then_inc(loaded, 16)
            sp.dma_start(raw_g[:, :, 0:D], expert_w.rearrange("(c p) n -> p c n", p=P)).then_inc(wg_loaded, 16)
            sp.dma_start(raw_g[:, :, D:YW], gate_w.rearrange("(c p) n -> p c n", p=P)).then_inc(wg_loaded, 16)
            sp.dma_start(raw_d[:], down_w.rearrange("(c p) n -> p c n", p=P)).then_inc(wd_loaded, 16)
            sp.dma_start(x[:, TC:2 * TC, :], rows(x_in, 1)).then_inc(x_loaded[0][1], 16)
            sp.dma_start(gam[:], gamma.rearrange("(a d) -> a d", a=1).broadcast_to([P, D])).then_inc(gb_loaded, 16)
            sp.dma_start(bet[:], beta.rearrange("(a d) -> a d", a=1).broadcast_to([P, D])).then_inc(gb_loaded, 16)
            for c in range(2, NC):
                sp.dma_start(x[:, TC * c:TC * c + TC, :], rows(x_in, c)).then_inc(x_loaded[0][c], 16)
            for m, w in enumerate((wqT, wkT, wvT)):
                sp.dma_start(raw_w[:, m], w.rearrange("(c p) n -> p c n", p=P)).then_inc(wp_loaded, 16)
            sp.dma_start(wo[:], woT.rearrange("g p n -> p g n")).then_inc(wo_loaded, 16)
            sp.wait_ge(w_hi, 4)
            sp.wait_ge(w_lo, 4)
            sp.dma_start(wall_d, wall[:].bitcast(F32)).then_inc(wall_stored, 16)
            for c in range(NC):
                sp.wait_ge(x_done, TC * (c + 1))
                sp.dma_start(rows(x1_d, c), x[:, TC * c:TC * c + TC, :]).then_inc(x1_stored[c], 16)
            sp.wait_ge(wall_stored, 16)
            sp.wait_ge(y_summed, FT)
            for c in range(NC):
                sp.wait_ge(x1_stored[c], 16)
            sp.wait_ge(ones_ready, 1)
            sp.dma_start(K[PARTS:PARTS + NSH].rearrange("r h (a s) -> r (h a) s", s=CH), ones[:].rearrange("r (a s) -> r a s", a=1).broadcast_to([NSH, H * NC, CH])).then_inc(ones_loaded, 16)
            for c in range(NC):
                for w in range(4):
                    n = 4 * c + w
                    m, hc = w // 2, w % 2
                    sp.wait_ge(part_l, n + 1)
                    sp.dma_start(part_d[m, :, hc * P:(hc + 1) * P, c * CH:(c + 1) * CH].rearrange("a d s -> d a s"),
                                 parts[:, n % NB]).then_inc(parts_stored[n % NB], 16)
                for k in range(NB):
                    sp.wait_ge(parts_stored[k], 16 * (c + 1))
                if c == 2:
                    sp.wait_ge(turned, 2 * NC)
                for r in range(6):
                    for m, dst, order in ((0, Q[:, c], (0, 0, 1, 1, 0, 2)), (1, K[:, :, c * CH:(c + 1) * CH], (0, 1, 0, 1, 2, 0))):
                        sp.dma_start(dst[r * DH:(r + 1) * DH],
                                     part_d[m, order[r], :, c * CH:(c + 1) * CH].rearrange("(h d) s -> d h s", d=DH)).then_inc(qk_loaded[c], 16)
            for u, (c, g) in enumerate(UNITS):
                if u == 0:
                    sp.wait_ge(vj_done, NT)
                    sp.dma_start(x1t[:], rows(x1_d, 0)).then_inc(x1t_loaded, 16)
                sp.wait_ge(acc_out, u + 1)
                sp.dma_start(den_d[u].rearrange("(j q) -> j q", j=G), att[DH:P:32, g, :]).then_inc(den_stored, 16)
                sp.wait_ge(den_stored, 16 * (u + 1))
                if u >= 2:
                    sp.wait_ge(inv_ready, u - 1)
                sp.dma_start(den[:, u % 2], den_d[u].rearrange("(p q) -> p q", p=32)).then_inc(den_loaded, 16)
                if u == NU - 1:
                    sp.wait_ge(qk_done, G * len(STEPS))
                    for k in (1, 2):
                        sp.wait_ge(x2_stored[k], 16)
                        sp.dma_start(x[:, TC * k:TC * k + TC, :], rows(x2_d, k)).then_inc(x_loaded[1][k], 16)
                    sp.dma_start(x[:, TC * (NC - 1):NT, :], rows(x1_d, NC - 1)).then_inc(x_loaded[1][NC - 1], 16)
                sp.wait_ge(inv_ready, u + 1)
                sp.dma_start(inv_d[u].rearrange("(p q) -> p q", p=32), inv[:, u % 2]).then_inc(inv_stored, 16)
                sp.wait_ge(inv_stored, 16 * (u + 1))
                if u >= 2:
                    sp.wait_ge(norm_done, u - 1)
                sp.dma_start(rb[:, u % 2], inv_d[u].rearrange("(j a q) -> j a q", j=G, a=1).broadcast_to([G, 32, CH])).then_inc(rb_loaded[u % 2], 16)
                if g == 0 and c:
                    sp.wait_ge(slot_free, PROJECTED[c - 1])
                    sp.dma_start(rows(x2_d, c - 1), x1t[:]).then_inc(x2_stored[c - 1], 16)
                    sp.wait_ge(x2_stored[c - 1], 16)
                    if c < NC - 1:
                        sp.dma_start(x1t[:], rows(x1_d, c)).then_inc(x1t_loaded, 16)
                if u == NU - NG:
                    sp.wait_ge(qk_done, G * FIRST[NU - NG])
                    sp.dma_start(x[:, 0:TC, :], rows(x2_d, 0)).then_inc(x_loaded[1][0], 16)
                    sp.dma_start(wall[:].bitcast(F32), wall_d).then_inc(wall_back, 16)
            for c in range(NC):
                sp.wait_ge(x_done, FT + TC * (c + 1))
                sp.dma_start(rows(out, c), x[:, TC * c:TC * c + TC, :]).then_inc(out_stored, 16)
            sp.wait_ge(out_stored, 16 * NC)

        @block.gpsimd
        def _(gp):
            count = [0]

            def link(ins):
                count[0] += 1
                ins.then_inc(pool, 1)
                gp.wait_ge(pool, count[0])

            nc.gpsimd.memset(ident[:], 0.0).then_inc(consts_ready, 1)
            nc.gpsimd.memset(mask[:], 0.0).then_inc(consts_ready, 1)
            gp.wait_ge(consts_ready, 2)
            nc.gpsimd.affine_select(out=ident[:], in_=ident[:], compare_op=ALU.not_equal, fill=1.0, base=0,
                                    pattern=[[-1, P]], channel_multiplier=1).then_inc(consts_ready, 1)
            nc.gpsimd.affine_select(out=mask[:], in_=mask[:], compare_op=ALU.is_ge, fill=LOWEST, base=0,
                                    pattern=[[-1, P]], channel_multiplier=1).then_inc(consts_ready, 1)

            def normalise(u):
                gp.wait_ge(rb_loaded[u % 2], 16 * (u // 2 + 1))
                gp.wait_ge(den_stored, 16 * (u + 1))
                at = att[:, UNITS[u][1]]
                nc.gpsimd.tensor_tensor(at, at, rb[:, u % 2], ALU.mult).then_inc(norm_done, 1)

            def add_output(v):
                gp.wait_ge(yh_ready, v + 1)
                link(nc.gpsimd.tensor_tensor(yh[:, v % 2], yh[:, v % 2], gam[:], ALU.mult))
                xt = x[:, v % NT]
                nc.gpsimd.tensor_tensor(xt, xt, yh[:, v % 2], ALU.add).then_inc(x_done, 1)

            def ffn(f):
                for c in range(NC):
                    n = NF * f + c
                    for i in range(IC):
                        u = IC * n + i
                        gp.wait_ge(relu_done, u + 1)
                        if u >= 2:
                            gp.wait_ge(lo_done, u - 1)
                        nc.gpsimd.tensor_tensor(sq[:, u % 2], relu[:, u % NR], relu[:, u % NR], ALU.mult).then_inc(sq_done, 1)
                    gp.wait_ge(gb_ready, 2)
                    for j in range(TC):
                        xt = x[:, TC * c + j]
                        nc.gpsimd.tensor_tensor(xt, xt, bet[:], ALU.add).then_inc(x_beta, 1)
                        if j:
                            add_output(TC * n + j - 1)
                    if n == NC:
                        normalise(NU - 1)

            ffn(0)
            gp.wait_ge(y_done, FT)
            gp.wait_ge(w_lo, 4)
            gp.wait_ge(w_hi, 4)
            nc.gpsimd.memset(V[:, :, :, DH:DH + 1], 1.0).then_inc(v_ones, 1)
            for n in range(4 * NC):
                gp.wait_ge(part_m, n + 1)
                nc.gpsimd.tensor_tensor(parts[:, n % NB, 2], rest[:, n % NRE], parts[:, n % NB, 1], ALU.subtract).then_inc(part_l, 1)
            for kind, what in PLAN:
                if kind == "exp" and what[1] == G - 1:
                    s = what[0]
                    u, kt = STEPS[s]
                    c = UNITS[u][0]
                    if kt >= TC * c:
                        q0 = P * (kt - TC * c)
                        gp.wait_ge(exp_done, G * (s + 1))
                        blk = pr[:, s % 3, :, q0:q0 + P]
                        nc.gpsimd.affine_select(out=blk, in_=blk, compare_op=ALU.is_ge, fill=0.0, base=0,
                                                pattern=[[0, G], [1, P]], channel_multiplier=-1).then_inc(sel_done, 1)
                elif kind == "norm" and what < NU - 1:
                    normalise(what)
            ffn(1)

        @block.scalar
        def _(act):
            def weight_hi(dst, src, loaded, n):
                act.wait_ge(loaded, n)
                nc.scalar.copy(dst, src).then_inc(w_hi, 1)

            def sqrt_of(c_no):
                act.wait_ge(mv_ready, c_no + 1)
                nc.scalar.activation(sd[:], mv[:, :, 1], ACT.Sqrt, bias=eps_t[:, 0:1]).then_inc(sd_ready, 1)

            def turned_hi(c_no, dst):
                act.wait_ge(turned, c_no + 1)
                nc.scalar.copy(dst, ps[:, 0:KC, :]).then_inc(xT_hi, 1)

            def turn_dst(t, part):
                return (xqT if NC <= t < 2 * NC else xT)[t % 2][part][:]

            def ffn(f):
                if not f:
                    sqrt_of(0)
                    weight_hi(wu[0][:, :, 0:IH], raw_u[:, :, 0:IH], wu_loaded, 16)
                turned_hi(2 * NC * f, turn_dst(0, 0))
                if not f:
                    weight_hi(wu[0][:, :, IH:I], raw_u[:, :, IH:I], wv_loaded, 16)

                def sqrt_of_tile(v):
                    act.wait_ge(mv2_ready, v + 1)
                    nc.scalar.activation(sd2[:, v % 2:v % 2 + 1], mv2[:, v % 2, 1:2], ACT.Sqrt, bias=eps_t[:, 0:1]).then_inc(sd2_ready, 1)

                def square(u):
                    act.wait_ge(relu_done, u + 1)
                    if u >= IC and u % IC == 0:
                        act.wait_ge(y_done, TC * (u // IC))
                    nc.scalar.activation(hT[0][:, u % IC], relu[:, u % NR], ACT.Square).then_inc(hi_done, 1)

                for c in range(NC):
                    n = NF * f + c
                    t = 2 * NC * f + c
                    following = t + 1 < 3 * NC
                    for i in range(IC):
                        u = IC * n + i
                        if n == 0 and i == 4:
                            weight_hi(wg[0], raw_g[:], wg_loaded, 32)
                            weight_hi(wd[0], raw_d[:], wd_loaded, 16)
                        if n == 1 and i == 4:
                            for m in range(3):
                                weight_hi(wp[m][0][:], raw_w[:, m], wp_loaded, 48)
                        act.wait_ge(up_done, u + 1)
                        if u >= NR:
                            act.wait_ge(sq_done, u - NR + 1)
                            act.wait_ge(hi_done, u - NR + 1)
                        nc.scalar.activation(relu[:, u % NR], ps[:, 2 + u % 2, :], ACT.Relu).then_inc(relu_done, 1)
                        if i:
                            square(u - 1)
                        if i == 0 and c:
                            sqrt_of_tile(TC * n - 1)
                    square(u)
                    for j in range(TC):
                        v = TC * n + j
                        act.wait_ge(route_ready, v + 1)
                        if v >= 2:
                            act.wait_ge(y_summed, v - 1)
                        nc.scalar.mul(moe[:, v % 2], ps[:, 6 + v % 2, 0:D], route[:, v % 2:v % 2 + 1]).then_inc(moe_scaled, 1)
                        if j == 0 and following:
                            sqrt_of(t + 1)
                        if j == TURN_AFTER + 1 and following:
                            if n >= 1:
                                act.wait_ge(y_done, TC * n)
                            turned_hi(t + 1, turn_dst(t + 1, 0))
                        if j:
                            sqrt_of_tile(v - 1)
                sqrt_of_tile(TC * (n + 1) - 1)

            act.wait_ge(eps_ready, 1)
            ffn(0)
            sqrt_of(NC + 1)
            for c in range(NC):
                following = c + 1 < NC

                def middle_part(n):
                    act.wait_ge(rest_done, n + 1)
                    nc.scalar.copy(parts[:, n % NB, 1], rest[:, n % NRE]).then_inc(part_m, 1)

                for w in range(4):
                    n = 4 * c + w
                    act.wait_ge(pj_done, n + 1)
                    if n >= NB:
                        act.wait_ge(parts_stored[n % NB], 16 * (n // NB))
                    nc.scalar.copy(parts[:, n % NB, 0], ps[:, PJ[n % 4], :]).then_inc(part_h, 1)
                    if w:
                        middle_part(n - 1)
                for j in range(TC):
                    t = TC * c + j
                    act.wait_ge(vj_done, t + 1)
                    if t == 0:
                        act.wait_ge(v_ones, 1)
                    nc.scalar.copy(V[:, t, :, 0:DH], ps[:, 4 + t % 2, 0:D].rearrange("p (h d) -> p h d", h=H)).then_inc(v_done, 1)
                    if j == 0:
                        middle_part(n)
                    if j == 2 and c + 2 < NC:
                        sqrt_of(NC + c + 2)
                    if j == 1 and following:
                        if c:
                            act.wait_ge(vj_done, TC * c)
                        turned_hi(NC + c + 1, turn_dst(NC + c + 1, 0))
            for k in range(NB):
                act.wait_ge(parts_stored[k], 16 * NC)
            act.wait_ge(vj_done, NT)
            for kind, what in PLAN:
                if kind == "exp":
                    s, j = what
                    e = G * s + j
                    u, kt = STEPS[s]
                    c = UNITS[u][0]
                    q0 = max(0, P * (kt - TC * c))
                    act.wait_ge(qk_done, e + 1)
                    if s >= 3 and j == 0:
                        act.wait_ge(pv_done, s - 2)
                    nc.scalar.activation(pr[:, s % 3, j, q0:CH], ps[:, e % 3, q0:CH], ACT.Exp, scale=SCALE).then_inc(exp_done, 1)
                elif kind == "norm_x":
                    sqrt_of(2 * NC)
                elif kind == "acc":
                    c, g = UNITS[what]
                    act.wait_ge(pv_done, FIRST[what + 1])
                    if c:
                        act.wait_ge(slot_full, PROJECTED[c - 1])
                    nc.scalar.copy(att[:, g], ps[:, 3, :]).then_inc(acc_out, 1)
                elif kind == "rows":
                    c, g = UNITS[what]
                    act.wait_ge(mrow_ready, what + 1)
                    for a in range(NSH):
                        act.dma_start(Q[PARTS + a:PARTS + a + 1, c, G * g:G * g + G, :].rearrange("o j (i q) -> o (j i) q", q=P),
                                      mrow[:, what % 2, a, :]).then_inc(m_loaded[what % 2], 16)
            ffn(1)

        @block.vector
        def _(v_):
            count = [0]

            def link(ins):
                count[0] += 1
                ins.then_inc(dve, 1)
                v_.wait_ge(dve, count[0])

            def weight_lo(dst, src, hi, n, loaded=None, value=0):
                v_.wait_ge(w_hi, n)
                nc.vector.tensor_tensor(dst, src, hi.bitcast(F32), ALU.subtract).then_inc(w_lo, 1)

            def ln_stats(t, j):
                c = t % NC
                if j == 0:
                    if NC <= t < 2 * NC:
                        v_.wait_ge(x_done, TC * (c + 1))
                    else:
                        v_.wait_ge(x_loaded[t // (2 * NC)][c], 16)
                    if t == 3 * NC - 1:
                        v_.wait_ge(slot_free, SLOTS + 2)
                nc.vector.bn_stats(stat[:, j], x[:, TC * c + j]).then_inc(stats_done, 1)

            def ln_mean(t):
                v_.wait_ge(stats_done, TC * (t + 1))
                for j in range(TC):
                    last = nc.vector.bn_aggr(mv[:, j], stat[:, j])
                last.then_inc(mv_ready, 1)

            def ln_rows(t):
                v_.wait_ge(sd_ready, t + 1)
                link(nc.vector.reciprocal(rs[:], sd[:]))
                if t >= 2:
                    v_.wait_ge(turned, t - 1)
                for j in range(TC):
                    last = nc.vector.tensor_scalar(xn[:, t % 2, j], x[:, TC * (t % NC) + j], mv[:, j, 0:1], rs[:, j:j + 1],
                                                   ALU.subtract, ALU.mult)
                last.then_inc(xn_ready, 1)

            def layer_norm(t):
                for j in range(TC):
                    ln_stats(t, j)
                ln_mean(t)
                ln_rows(t)

            def turn_dst(t, part):
                return (xqT if NC <= t < 2 * NC else xT)[t % 2][part][:]

            def turned_lo(t):
                v_.wait_ge(xT_hi, t + 1)
                nc.vector.tensor_tensor(turn_dst(t, 1), ps[:, 0:KC, :], turn_dst(t, 0).bitcast(F32), ALU.subtract).then_inc(xT_lo, 1)

            def halve_gamma_beta():
                v_.wait_ge(gb_loaded, 32)
                nc.vector.tensor_scalar(gam[:], gam[:], 0.5, None, ALU.mult).then_inc(gb_ready, 1)
                nc.vector.tensor_scalar(bet[:], bet[:], 0.5, None, ALU.mult).then_inc(gb_ready, 1)

            def ffn(f):
                first = 2 * NC * f
                if not f:
                    layer_norm(0)
                    weight_lo(wu[1][:, :, 0:IH], raw_u[:, :, 0:IH], wu[0][:, :, 0:IH], 1)
                turned_lo(first)
                if not f:
                    weight_lo(wu[1][:, :, IH:I], raw_u[:, :, IH:I], wu[0][:, :, IH:I], 2)

                def normalised(v):
                    k = v % 2
                    v_.wait_ge(sd2_ready, v + 1)
                    link(nc.vector.reciprocal(rs2[:, k:k + 1], sd2[:, k:k + 1]))
                    if v >= 2:
                        v_.wait_ge(x_done, v - 1)
                    nc.vector.tensor_scalar(yh[:, k], y[:, k], mv2[:, k, 0:1], rs2[:, k:k + 1], ALU.subtract, ALU.mult).then_inc(yh_ready, 1)
                    if v % TC == TC - 1:
                        v_.wait_ge(yh_ready, v + 1)
                        link(nc.vector.tensor_tensor(yh[:, k], yh[:, k], gam[:], ALU.mult))
                        v_.wait_ge(x_beta, v + 1)
                        nc.vector.tensor_tensor(x[:, v % NT], x[:, v % NT], yh[:, k], ALU.add).then_inc(x_done, 1)

                for c in range(NC):
                    n = NF * f + c
                    t = first + c
                    following = t + 1 < 3 * NC
                    for i in range(IC):
                        u = IC * n + i
                        if n == 0 and i == 4:
                            weight_lo(wg[1], raw_g[:], wg[0], 3)
                            weight_lo(wd[1], raw_d[:], wd[0], 4)
                        if n == 1 and i == 4:
                            for m in range(3):
                                weight_lo(wp[m][1][:], raw_w[:, m], wp[m][0][:], 5 + m)
                        v_.wait_ge(hi_done, u + 1)
                        v_.wait_ge(sq_done, u + 1)
                        nc.vector.tensor_tensor(hT[1][:, i], sq[:, u % 2], hT[0][:, i].bitcast(F32), ALU.subtract).then_inc(lo_done, 1)
                        if i == 0 and c:
                            normalised(TC * n - 1)
                        if n == 0 and i == 3:
                            halve_gamma_beta()
                        if n == NC and i == 2:
                            inverse(NU - 1)
                        if n == NC + 1 and i == LAST_PROJ:
                            projected(NC - 1, 0, SLOTS)
                            projected(NC - 1, 1, SLOTS + 1)
                        if following and STATS_AT <= i < STATS_AT + TC:
                            ln_stats(t + 1, i - STATS_AT)
                        if following and i == IC - 1:
                            ln_mean(t + 1)
                    for j in range(TC):
                        v = TC * n + j
                        k = v % 2
                        v_.wait_ge(moe_done, v + 1)
                        link(nc.vector.max(top8[:], ps[:, 6 + k, D:YW]))
                        nc.vector.tensor_tensor(route[:, k:k + 1], top8[:, 0:1], top8[:, 1:2], ALU.add).then_inc(route_ready, 1)
                        if j:
                            normalised(v - 1)
                        if j == 0 and following:
                            ln_rows(t + 1)
                        v_.wait_ge(moe_scaled, v + 1)
                        v_.wait_ge(y_done, v + 1)
                        nc.vector.tensor_tensor(y[:, k], ps[:, 4 + k, 0:D], moe[:, k], ALU.add).then_inc(y_summed, 1)
                        if j == TURN_AFTER + 1 and following:
                            turned_lo(t + 1)
                        v_.wait_ge(y_summed, v + 1)
                        link(nc.vector.bn_stats(stat2[:], y[:, k]))
                        nc.vector.bn_aggr(mv2[:, k], stat2[:]).then_inc(mv2_ready, 1)
                normalised(TC * (n + 1) - 1)

            def inverse(u):
                v_.wait_ge(den_loaded, 16 * (u + 1))
                if u >= 2:
                    v_.wait_ge(inv_stored, 16 * (u - 1))
                nc.vector.reciprocal(inv[:, u % 2], den[:, u % 2]).then_inc(inv_ready, 1)

            def projected(c, half, z):
                v_.wait_ge(slot_full, z + 1)
                if c < NC - 1:
                    v_.wait_ge(x1t_loaded, 16 * (c + 1))
                    xt = x1t[:, 2 * half:2 * half + 2, :]
                else:
                    v_.wait_ge(x_loaded[1][c], 16)
                    xt = x[:, TC * c + 2 * half:TC * c + 2 * half + 2, :]
                nc.vector.tensor_tensor(xt, ps[:, 4 + 2 * (z % 2):6 + 2 * (z % 2), 0:D], xt, ALU.add).then_inc(slot_free, 1)

            nc.vector.memset(eps_t[:], EPS).then_inc(eps_ready, 1)
            nc.vector.memset(ones[:], 1.0).then_inc(ones_ready, 1)
            nc.vector.memset(mxp[:], LOWEST).then_inc(at_start, 1)
            v_.wait_ge(at_start, 1)
            ffn(0)
            layer_norm(NC + 1)
            for c in range(NC):
                t = NC + c
                following = c + 1 < NC
                for w in range(4):
                    n = 4 * c + w
                    v_.wait_ge(part_h, n + 1)
                    if n >= NRE:
                        v_.wait_ge(part_l, n - NRE + 1)
                    nc.vector.tensor_tensor(rest[:, n % NRE], ps[:, PJ[n % 4], :], parts[:, n % NB, 0], ALU.subtract).then_inc(rest_done, 1)
                if following:
                    turned_lo(t + 1)
                if c + 2 < NC:
                    layer_norm(t + 2)
            nc.vector.memset(ps[:, 3, :], 0.0).then_inc(at_start, 1)
            v_.wait_ge(part_l, 4 * NC)
            v_.wait_ge(consts_ready, 4)
            for event in PLAN:
                kind, what = event
                if kind == "max":
                    z = SLOT[event]
                    slot = ps[:, 4 + 2 * (z % 2):6 + 2 * (z % 2), :]
                    u, i, ch, pair = PIECES[what]
                    c = UNITS[u][0]
                    mx = mxp[:, u % 3]
                    v_.wait_ge(slot_full, z + 1)
                    if (i, ch, pair) == (0, 0, 0) and u >= 3:
                        v_.wait_ge(top_ready, u - 2)
                    off = CH if ch < c else P * i
                    if off:
                        last = nc.vector.tensor_reduce(mx[:, ch + 1, 2 * pair:2 * pair + 2, i], slot[:, :, 0:off], AX.X, ALU.max)
                    if ch == c:
                        for k in range(2):
                            blk = slot[:, k, P * i:P * i + P]
                            last = nc.vector.tensor_tensor_reduce(blk, blk, mask[:], 1.0, LOWEST, ALU.add, ALU.max,
                                                                  mx[:, 0, 2 * pair + k, i:i + 1])
                    last.then_inc(slot_free, 1)
                elif kind == "top":
                    c = UNITS[what][0]
                    v_.wait_ge(slot_free, SLOT[("max", LAST_PIECE[what])] + 1)
                    nc.vector.tensor_reduce(mcol[:, what % 2], mxp[:, what % 3, 0:c + 2].rearrange("p s j i -> p (j i) s"), AX.X,
                                            ALU.max).then_inc(top_ready, 1)
                elif kind == "turn":
                    z = SLOT[event]
                    b = what % 2
                    src = ps[0:G * TC, 4 + 2 * (z % 2), 0:P]
                    v_.wait_ge(slot_full, z + 1)
                    if what >= 2:
                        v_.wait_ge(m_loaded[b], 16 * NSH * (what // 2))
                    link(nc.vector.tensor_scalar(mrow[:, b, 0], src, -1.0, None, ALU.mult))
                    nc.vector.scalar_tensor_tensor(out=mrest[:, b], in0=src, scalar=-1.0, in1=mrow[:, b, 0],
                                                   op0=ALU.mult, op1=ALU.subtract).then_inc(slot_free, 1)
                    v_.wait_ge(slot_free, z + 1)
                    link(nc.vector.tensor_copy(mrow[:, b, 1], mrest[:, b]))
                    nc.vector.tensor_tensor(mrow[:, b, 2], mrest[:, b], mrow[:, b, 1], ALU.subtract).then_inc(mrow_ready, 1)
                elif kind == "inv":
                    if what < NU - 1:
                        inverse(what)
                elif kind == "proj":
                    projected(*what, SLOT[event])
                elif kind == "norm_x":
                    layer_norm(2 * NC)
            ffn(1)

        @block.tensor
        def _(pe):
            def turn(t):
                src = xn[:, t % 2]
                pe.wait_ge(xn_ready, t + 1)
                if t:
                    pe.wait_ge(xT_hi, t)
                    pe.wait_ge(xT_lo, t)
                for j in range(TC):
                    for k in range(KC):
                        mm = nc.tensor.transpose(ps[:, k, P * j:P * j + P], src[:, j, P * k:P * k + P], ident[:])
                mm.then_inc(turned, 1)

            def product(dst, lhs, rhs, chunks):
                n = 0
                for k in chunks:
                    for a, b in ((0, 0), (0, 1), (1, 0)):
                        mm = nc.tensor.matmul(dst, lhs(a, k), rhs(b, k), start=(n == 0), stop=(n == 3 * len(chunks) - 1))
                        n += 1
                return mm

            def ffn(f):
                first = 2 * NC * f
                if f:
                    pe.wait_ge(exp_done, G * len(STEPS))
                    pe.wait_ge(acc_out, NU)
                    pe.wait_ge(wall_back, 16)
                turn(first)
                for c in range(NC):
                    n = NF * f + c
                    xt = xT[c % 2]
                    t = first + c
                    pe.wait_ge(xT_hi, t + 1)
                    pe.wait_ge(xT_lo, t + 1)
                    for i in range(IC):
                        u = IC * n + i
                        if n == 0 and i % 4 == 0:
                            pe.wait_ge(w_hi, 1 + i // 4)
                            pe.wait_ge(w_lo, 1 + i // 4)
                        if u >= 2:
                            pe.wait_ge(relu_done, u - 1)
                        product(ps[:, 2 + u % 2, :], lambda a, k: wu[a][:, k, P * i:P * i + P], lambda b, k: xt[b][:, k, :],
                                range(KC)).then_inc(up_done, 1)
                        if n == NC + 1 and i == LAST_PROJ:
                            project(NC - 1, 0, SLOTS)
                            project(NC - 1, 1, SLOTS + 1)
                    if n == 0:
                        pe.wait_ge(w_hi, 4)
                        pe.wait_ge(w_lo, 4)
                    if n == NC:
                        pe.wait_ge(slot_free, SLOTS)
                    if n == NC + 1:
                        pe.wait_ge(slot_free, SLOTS + 2)
                    for j in range(TC):
                        v = TC * n + j
                        if v >= 2:
                            pe.wait_ge(moe_scaled, v - 1)
                            pe.wait_ge(y_summed, v - 1)
                            pe.wait_ge(route_ready, v - 1)
                        product(ps[:, 6 + v % 2, 0:YW], lambda a, k: xt[a][:, k, P * j:P * j + P], lambda b, k: wg[b][:, k, :],
                                range(KC)).then_inc(moe_done, 1)
                        for i in range(IC):
                            if j == 0:
                                pe.wait_ge(lo_done, IC * n + i + 1)
                            for m, (a, b) in enumerate(((0, 0), (0, 1), (1, 0))):
                                mm = nc.tensor.matmul(ps[:, 4 + v % 2, 0:D], hT[a][:, i, P * j:P * j + P], wd[b][:, i, :],
                                                      start=(i == 0 and m == 0), stop=(i == IC - 1 and m == 2))
                        mm.then_inc(y_done, 1)
                        if j == TURN_AFTER and t + 1 < 3 * NC:
                            turn(t + 1)

            def project(c, half, z):
                pe.wait_ge(slot_free, z - 1)
                if c == NC - 1:
                    pe.wait_ge(moe_scaled, TC * (NC + 1))
                    pe.wait_ge(y_summed, TC * (NC + 1))
                    pe.wait_ge(route_ready, TC * (NC + 1))
                pe.wait_ge(norm_done, NG * (c + 1))
                for k in range(2):
                    t = 2 * half + k
                    for g in range(NG):
                        mm = nc.tensor.matmul(ps[:, 4 + 2 * (z % 2) + k, 0:D], att[:, g, P * t:P * t + P], wo[:, g, :],
                                              start=(g == 0), stop=(g == NG - 1))
                mm.then_inc(slot_full, 1)

            pe.wait_ge(consts_ready, 4)
            ffn(0)
            pe.wait_ge(w_hi, 7)
            pe.wait_ge(w_lo, 7)
            for c in range(NC):
                t = NC + c
                if c == 0:
                    pe.wait_ge(relu_done, IC * NF)
                    pe.wait_ge(y_summed, FT)
                pe.wait_ge(xT_hi, t + 1)
                pe.wait_ge(xT_lo, t + 1)
                xt = xqT[c % 2]
                for w in range(4):
                    n = 4 * c + w
                    m, hc = w // 2, w % 2
                    if n >= 4:
                        pe.wait_ge(rest_done, n - 3)
                    product(ps[:, PJ[n % 4], :], lambda a, k: wp[m][a][:, k, P * hc:P * hc + P], lambda b, k: xt[b][:, k, :],
                            range(KC)).then_inc(pj_done, 1)
                for j in range(TC):
                    if j == 0 and c + 1 < NC:
                        turn(NC + c + 1)
                    t = TC * c + j
                    if t >= 2:
                        pe.wait_ge(v_done, t - 1)
                    product(ps[:, 4 + t % 2, 0:D], lambda a, k: xt[a][:, k, P * j:P * j + P], lambda b, k: wp[2][b][:, k, :],
                            range(KC)).then_inc(vj_done, 1)
            pe.wait_ge(v_done, NT)
            pe.wait_ge(part_l, 4 * NC)
            pe.wait_ge(at_start, 2)
            pe.wait_ge(ones_loaded, 16)
            pe.wait_ge(wo_loaded, 16)
            for event in PLAN:
                kind, what = event
                if kind == "max":
                    z = SLOT[event]
                    u, i, ch, pair = PIECES[what]
                    c, g = UNITS[u]
                    if z >= 2:
                        pe.wait_ge(slot_free, z - 1)
                    if (g, i, ch, pair) == (0, 0, 0, 0):
                        pe.wait_ge(qk_loaded[c], 16 * 12)
                    w = CH if ch < c else P * (i + 1)
                    for k in range(2):
                        h = G * g + 2 * pair + k
                        mm = nc.tensor.matmul(ps[:, 4 + 2 * (z % 2) + k, 0:w], Q[0:PARTS, c, h, P * i:P * i + P],
                                              K[0:PARTS, h, CH * ch:CH * ch + w], start=True, stop=True)
                    mm.then_inc(slot_full, 1)
                elif kind == "turn":
                    z = SLOT[event]
                    pe.wait_ge(slot_free, z - 1)
                    pe.wait_ge(top_ready, what + 1)
                    nc.tensor.transpose(ps[0:G * TC, 4 + 2 * (z % 2), 0:P], mcol[:, what % 2], ident[:]).then_inc(slot_full, 1)
                elif kind == "exp":
                    s, j = what
                    e = G * s + j
                    u, kt = STEPS[s]
                    c, g = UNITS[u]
                    if e >= 3:
                        pe.wait_ge(exp_done, e - 2)
                    if kt == 0 and j == 0:
                        pe.wait_ge(m_loaded[u % 2], 16 * NSH * (u // 2 + 1))
                    q0 = max(0, P * (kt - TC * c))
                    h = G * g + j
                    nc.tensor.matmul(ps[:, e % 3, q0:CH], K[0:PARTS + NSH, h, P * kt:P * kt + P], Q[0:PARTS + NSH, c, h, q0:CH],
                                     start=True, stop=True).then_inc(qk_done, 1)
                elif kind == "pv":
                    s = what
                    u, kt = STEPS[s]
                    c, g = UNITS[u]
                    q0 = max(0, P * (kt - TC * c))
                    pe.wait_ge(exp_done, G * (s + 1))
                    if kt >= TC * c:
                        pe.wait_ge(sel_done, DIAG[s + 1])
                    if kt == 0 and u:
                        pe.wait_ge(acc_out, u)
                    for j in range(G):
                        mm = nc.tensor.matmul(ps[32 * j:32 * j + DH + 1, 3, q0:CH], V[:, kt, G * g + j, :], pr[:, s % 3, j, q0:CH],
                                              start=(kt == 0), stop=(kt == TC * c + TC - 1))
                    mm.then_inc(pv_done, 1)
                elif kind == "proj":
                    project(*what, SLOT[event])
            ffn(1)


def kernel(L0_attn_x, L0_attn_Wq, L0_attn_Wk, L0_attn_Wv, L0_attn_Wo, L0_ffn_gate_w, L0_ffn_up_w, L0_ffn_down_w,
           L0_ffn_expert_weight, L0_ffn_ln_gamma, L0_ffn_ln_beta):
    import numpy as np
    import concourse.bacc as bacc
    from concourse.bass_utils import run_bass_kernel_spmd

    wo = np.asarray(L0_attn_Wo)
    woT = np.zeros((NG, G, 32, D), wo.dtype)
    woT[:, :, :DH, :] = wo.T.reshape(NG, G, DH, D)
    arrays = {
        "x": np.asarray(L0_attn_x).reshape(S, D),
        "wqT": np.ascontiguousarray(np.asarray(L0_attn_Wq).T),
        "wkT": np.ascontiguousarray(np.asarray(L0_attn_Wk).T),
        "wvT": np.ascontiguousarray(np.asarray(L0_attn_Wv).T),
        "woT": woT.reshape(NG, P, D),
        "gate_w": np.ascontiguousarray(L0_ffn_gate_w),
        "up_w": np.ascontiguousarray(L0_ffn_up_w),
        "down_w": np.ascontiguousarray(L0_ffn_down_w),
        "expert_w": np.ascontiguousarray(L0_ffn_expert_weight),
        "gamma": np.ascontiguousarray(L0_ffn_ln_gamma),
        "beta": np.ascontiguousarray(L0_ffn_ln_beta),
    }
    nc = bacc.Bacc("TRN2", target_bir_lowering=False, num_devices=1)
    args = [nc.dram_tensor(f"in_{n}", a.shape, mybir.dt.from_np(a.dtype), kind="ExternalInput").ap() for n, a in arrays.items()]
    res = nc.dram_tensor("res", (S, D), F32, kind="ExternalOutput").ap()
    build(nc, *args, res)
    r = run_bass_kernel_spmd(nc, [{f"in_{n}": a for n, a in arrays.items()}], core_ids=[0])
    return r.results[0]["res"].reshape(1, S, D)
```

```python
from contextlib import ExitStack

from concourse import mybir

F32 = mybir.dt.float32
F32R = mybir.dt.float32r
BF16 = mybir.dt.bfloat16
ALU = mybir.AluOpType
ACT = mybir.ActivationFunctionType
AX = mybir.AxisListType

P = 128
S = 2048
D = 256
I = 1024
E = 8
H = 16
DH = D // H
KC = D // P
IC = I // P
CH = 512
NC = S // CH
TC = CH // P
NT = S // P
IH = I // 2
G = 4
NG = H // G
YW = D + E
PARTS = 6 * DH
NSH = 3
EPS = 1e-5
LOWEST = -3.0e38
SCALE = float(DH) ** -0.5
KB = 1024
NR = 2
NRE = 2
NB = 4
PJ = (2, 3, 6, 7)

UNITS = [(c, g) for c in range(NC) for g in range(NG)]
NU = len(UNITS)
STEPS = [(u, kt) for u, (c, g) in enumerate(UNITS) for kt in range(TC * c + TC)]
FIRST = [sum(TC * c + TC for c, _ in UNITS[:u]) for u in range(NU + 1)]
PIECES = [(u, i, ch, j) for u, (c, g) in enumerate(UNITS) for i in range(TC) for ch in range(c + 1) for j in range(G)]

SLOT_BANKS = 4

WARM = 32
STATS_AT = 2
TURN_AFTER = 1
TURN_W = 2
STACK0 = 1
LAST_PROJ = 2
LAG = 2
LEAD = 6
PRO = 34
DIAG_COST = 200
TURNING = 3
SENDING = 7
SEL_AT = 1
INV_AT = 2
NORM_AT = 5
PROJ_AT = 6
TURN_X = 1


def attention_plan():
    plan = []
    done = 0
    later, turning, sending = {}, {}, {}

    def width(s):
        u, kt = STEPS[s]
        return CH - max(0, P * (kt - TC * UNITS[u][0]))

    step_cost = [G * (2 * width(s) + 60) for s in range(len(STEPS))]
    piece_cost = []
    for u, i, ch, j in PIECES:
        piece_cost.append(CH + 60 if ch < UNITS[u][0] else P * (i + 1) + DIAG_COST)

    def at(step, *event):
        later.setdefault(step, []).append(event)

    def turns():
        for w in list(turning):
            turning[w] -= 1
            if turning[w] <= 0 or done == len(PIECES):
                plan.append(("turn", w))
                del turning[w]
                sending[w] = SENDING

    def piece():
        nonlocal done
        u = PIECES[done][0]
        plan.append(("max", done))
        done += 1
        turns()
        if done == len(PIECES) or PIECES[done][0] != u:
            plan.append(("top", u))
            turning[u] = TURNING

    def tick(force=False):
        if done == len(PIECES):
            turns()
        for w in list(sending):
            sending[w] -= 1
            if not sending[w] or force:
                plan.append(("rows", w))
                del sending[w]

    for u, (c, g) in enumerate(UNITS):
        at(FIRST[u + 1] + LAG + INV_AT, "inv", u)
        if g % 2:
            at(FIRST[u + 1] + LAG + NORM_AT, "norm", u)
        if g == NG - 1 and c < NC - 1:
            for k in range(TC):
                at(FIRST[u + 1] + LAG + PROJ_AT + k, "proj", (c, k))
    while done < PRO:
        piece()
    tick(True)
    for s, (u, kt) in enumerate(STEPS):
        start, end = FIRST[u], FIRST[u + 1]
        if kt == 0:
            goal = min(len(PIECES), G * (FIRST[min(u + 2, NU)] + LEAD)) if u + 1 < NU else len(PIECES)
            ahead = sum(piece_cost[done:goal])
            total = sum(step_cost[start:end - (LEAD if u == NU - 2 else 0)])
            spent = 0
            given = 0
        for j in range(G):
            plan.append(("exp", (s, j)))
            tick()
            if j == 2 and s >= LAG:
                plan.append(("pv", s - LAG))
            spent += step_cost[s] / G
            if j == 3 and s >= LAG and STEPS[s - LAG + 1][0] != STEPS[s - LAG][0]:
                plan.append(("acc", STEPS[s - LAG][0]))
            while done < goal and given + piece_cost[done] / 2 <= ahead * spent / total:
                given += piece_cost[done]
                piece()
        if s == end - 1:
            while done < goal:
                piece()
        plan.extend(later.pop(s, []))
        if s == FIRST[NU - 2]:
            plan.append(("norm_x", None))
    for s in range(len(STEPS) - LAG, len(STEPS)):
        if s == len(STEPS) - TURN_X:
            plan.append(("turn_x", None))
        plan.append(("pv", s))
    plan.append(("acc", NU - 1))
    for s in sorted(later):
        plan.extend(later[s])
    return plan


PLAN = attention_plan()


def slots_of(plan):
    uses = [e for e in plan if e[0] in ("max", "turn", "proj")]
    return {e: z for z, e in enumerate(uses)}


SLOT = slots_of(PLAN)
PROJECTED = [SLOT[("proj", (c, TC - 1))] + 1 for c in range(NC - 1)]
SLOTS = len(SLOT)
LAST_PIECE = [max(n for n, p in enumerate(PIECES) if p[0] == u) for u in range(NU)]
EARLY = 2 * (4 + TC)
EARLY_EVENTS = [[]]
for n_events, planned in enumerate(PLAN):
    EARLY_EVENTS[-1].append(planned)
    if planned in SLOT:
        if SLOT[planned] == EARLY - 1:
            break
        if SLOT[planned] % 2:
            EARLY_EVENTS.append([])
MAIN = n_events + 1


def bank_of(z):
    return z % 2 if z < EARLY else 8 - SLOT_BANKS + z % SLOT_BANKS


def build(nc, x_in, wqT, wkT, wvT, woT, gate_w, up_w, down_w, expert_w, gamma, beta, out):
    def at(name, kb, shape, dt):
        return nc.alloc_sbuf_tensor_at(name, shape, dt, offset=16512 + int(kb * KB))

    with ExitStack() as ctx:
        def sem(name):
            return ctx.enter_context(nc.semaphore(name))

        ident = at("ident", 0, [P, P], F32)
        mask = at("mask", 3, [P, CH], F32)
        wo = at("wo", 1, [P, KC, D], F32)
        gam = at("gam", 5, [P, D], F32)
        bet = at("bet", 6, [P, D], F32)
        small = 7 * KB

        def tiny(name, shape, dt=F32):
            nonlocal small
            size = 4 if dt == F32 else 2
            for k in shape[1:]:
                size *= k
            t = at(name, small / KB, shape, dt)
            small += -(-size // 32) * 32
            return t

        eps_t = tiny("eps_t", [P, 1])
        stat = tiny("stat", [P, TC, 6])
        mv = tiny("mv", [P, TC, 2])
        sd = tiny("sd", [P, TC])
        rs = tiny("rs", [P, TC])
        stat2 = tiny("stat2", [P, 6])
        mv2 = tiny("mv2", [P, 2, 2])
        sd2 = tiny("sd2", [P, 2])
        rs2 = tiny("rs2", [P, 2])
        top8 = tiny("top8", [P, 8])
        scratch = tiny("scratch", [P, 1])
        route = tiny("route", [P, 2])
        assert small <= 8 * KB
        WU, WD, WG = KC * I, IC * D, KC * YW
        wall = at("wall", 8, [P, 2 * (WU + WD + WG)], F32R)
        wu = [wall[:, k * WU:(k + 1) * WU].rearrange("p (c n) -> p c n", c=KC) for k in range(2)]
        o = 2 * WU
        wd = [wall[:, o + k * WD:o + (k + 1) * WD].rearrange("p (c n) -> p c n", c=IC) for k in range(2)]
        o += 2 * WD
        wg = [wall[:, o + k * WG:o + (k + 1) * WG].rearrange("p (c n) -> p c n", c=KC) for k in range(2)]
        x = at("x", 52.125, [P, NT, D], F32)
        xn = at("xn", 44.125, [P, 2, TC, D], F32)
        xT = [[at(f"xT{b}{k}", 68.5 + 8 * b + 4 * k, [P, KC, CH], F32R) for k in range(2)] for b in range(2)]
        hT = [at(f"hT{k}", 85 + 16 * k, [P, IC, CH], F32R) for k in range(2)]
        relu = at("relu", 117, [P, NR, CH], F32)
        sq = at("sq", 121, [P, 2, CH], F32)
        moe = at("moe", 125, [P, 2, D], F32)
        y = at("y", 127, [P, 2, D], F32)
        yh = at("yh", 129, [P, 2, D], F32)
        raw_u = at("raw_u", 133, [P, KC, I], F32)
        raw_d = at("raw_d", 141, [P, IC, D], F32)
        raw_g = at("raw_g", 149, [P, KC, YW], F32)
        wp = [[at(f"wp{m}{k}", 154 + 4 * m + 2 * k, [P, KC, D], F32R) for k in range(2)] for m in range(3)]
        xqT = [[at(f"xqT{b}{k}", 178 + 8 * b + 4 * k, [P, KC, CH], F32R) for k in range(2)] for b in range(2)]
        parts = at("parts", 166, [P, NB, 3, CH], BF16)
        rest = at("rest", 194, [P, NRE, CH], F32)
        Q = at("Q", 8.125, [P, NC, H, CH], BF16)
        K = at("K", 72.125, [P, H, S], BF16)
        V = at("V", 136.125, [P, NT, H, DH + 1], F32)
        pr = at("pr", 154, [P, 3, G, CH], F32)
        sums = at("sums", 178, [P, 2, CH], F32)
        att = at("att", 182, [P, KC, CH], F32)
        rb = at("rb", 186, [P, 2, CH], F32)
        x1t = at("x1t", 190, [P, TC, D], F32)
        mrow = at("mrow", 194, [G * TC, 2, NSH, P], BF16)
        mrest = at("mrest", 195.5, [G * TC, 2, P], F32)
        den = at("den", 196.5, [P, 2, G * CH // P], F32)
        inv = at("inv", 197, [P, 2, G * CH // P], F32)
        raw_w = at("raw_w", 198, [P, 3, KC, D], F32)
        mxp = at("mxp", 204, [P, 3, NC, G, TC], F32)
        neg = at("neg", 206.5, [G * TC, 2, P], F32)
        mcol = at("mcol", 205, [P, 2, G * TC], F32)
        ones = at("ones", 205.25, [NSH, CH], BF16)

        ps = ctx.enter_context(nc.psum_tensor("ps", [P, 8, CH], F32))

        wall_d = nc.dram_tensor("wall_d", (P, 2 * (WU + WD + WG)), F32).ap()
        x1_d = nc.dram_tensor("x1_d", (S, D), F32).ap()
        x2_d = nc.dram_tensor("x2_d", (S, D), F32).ap()
        part_d = nc.dram_tensor("part_d", (2, 3, D, S), BF16).ap()
        sums_d = nc.dram_tensor("sums_d", (NU, G, 32, CH), F32).ap()
        inv_d = nc.dram_tensor("inv_d", (NU, G * CH), F32).ap()

        def rows(ap, c):
            return ap[c * CH:(c + 1) * CH, :].rearrange("(t p) d -> p t d", p=P)

        tile_loaded = [sem(f"tile_loaded{k}") for k in range(TC)]
        x_loaded = [[sem(f"x_loaded{f}{c}") for c in range(NC)] for f in range(2)]
        wu_loaded, wu2_loaded, wd_loaded, wg_loaded = (sem(n) for n in ("wu_loaded", "wu2_loaded", "wd_loaded", "wg_loaded"))
        wp_loaded, wo_loaded, gb_loaded = (sem(n) for n in ("wp_loaded", "wo_loaded", "gb_loaded"))
        consts_ready = sem("consts_ready")
        w_hi, w_lo = sem("w_hi"), sem("w_lo")
        wall_stored, wall_back = sem("wall_stored"), sem("wall_back")
        gb_ready = sem("gb_ready")
        eps_ready = sem("eps_ready")
        act_own = sem("act_own")
        dve = sem("dve")
        pool = sem("pool")
        stats_done, mv_ready, sd_ready, xn_ready = sem("stats_done"), sem("mv_ready"), sem("sd_ready"), sem("xn_ready")
        turned, xT_hi, xT_lo = sem("turned"), sem("xT_hi"), sem("xT_lo")
        up_done, relu_done, sq_done, hi_done = (sem(n) for n in ("up_done", "relu_done", "sq_done", "hi_done"))
        lo_done = sem("lo_done")
        moe_done, y_done = sem("moe_done"), sem("y_done")
        route_ready, moe_scaled, y_summed = sem("route_ready"), sem("moe_scaled"), sem("y_summed")
        mv2_ready, sd2_ready, yh_ready, x_beta = (sem(n) for n in ("mv2_ready", "sd2_ready", "yh_ready", "x_beta"))
        x_done = sem("x_done")
        x1_stored = [sem(f"x1_stored{c}") for c in range(NC)]
        x2_stored = [sem(f"x2_stored{c}") for c in range(NC)]
        out_stored = sem("out_stored")
        pj_done, part_h, rest_done, part_m = (sem(n) for n in ("pj_done", "part_h", "rest_done", "part_m"))
        part_l = sem("part_l")
        vj_done, v_done, v_ones = sem("vj_done"), sem("v_done"), sem("v_ones")
        parts_stored = [sem(f"parts_stored{k}") for k in range(NB)]
        qk_loaded = [sem(f"qk_loaded{c}") for c in range(NC)]
        ones_ready, ones_loaded = sem("ones_ready"), sem("ones_loaded")
        acc_zeroed = sem("acc_zeroed")
        slot_full, slot_free = sem("slot_full"), sem("slot_free")
        top_ready, mrow_ready = sem("top_ready"), sem("mrow_ready")
        m_loaded = [sem(f"m_loaded{k}") for k in range(2)]
        qk_done, exp_done, sel_done, pv_done = (sem(n) for n in ("qk_done", "exp_done", "sel_done", "pv_done"))
        acc_out = sem("acc_out")
        sums_stored, den_loaded, inv_ready, inv_stored = (sem(n) for n in ("sums_stored", "den_loaded", "inv_ready", "inv_stored"))
        norm_done = sem("norm_done")
        att_loaded = [sem(f"att_loaded{k}") for k in range(NG)]
        rb_loaded = [sem(f"rb_loaded{k}") for k in range(NG)]
        x1t_loaded = sem("x1t_loaded")

        NF = NC
        FT = NC * TC

        def diag_before(s):
            return sum(1 for u, kt in STEPS[:s] if kt >= TC * UNITS[u][0])

        DIAG = [diag_before(s) for s in range(len(STEPS) + 1)]
        block = ctx.enter_context(nc.Block())

        @block.sync
        def _(sp):
            for k in range(TC):
                sp.dma_start(x[:, k, :], x_in[k * P:(k + 1) * P, :]).then_inc(tile_loaded[k], 16)
            for k, loaded in enumerate((wu_loaded, wu2_loaded)):
                sp.dma_start(raw_u[:, :, k * IH:(k + 1) * IH], up_w.rearrange("(c p) n -> p c n", p=P)[:, :, k * IH:(k + 1) * IH]).then_inc(loaded, 16)
            sp.dma_start(raw_g[:, :, 0:D], expert_w.rearrange("(c p) n -> p c n", p=P)).then_inc(wg_loaded, 16)
            sp.dma_start(raw_g[:, :, D:YW], gate_w.rearrange("(c p) n -> p c n", p=P)).then_inc(wg_loaded, 16)
            sp.dma_start(raw_d[:], down_w.rearrange("(c p) n -> p c n", p=P)).then_inc(wd_loaded, 16)
            sp.dma_start(x[:, TC:2 * TC, :], rows(x_in, 1)).then_inc(x_loaded[0][1], 16)
            sp.dma_start(gam[:], gamma.rearrange("(a d) -> a d", a=1).broadcast_to([P, D])).then_inc(gb_loaded, 16)
            sp.dma_start(bet[:], beta.rearrange("(a d) -> a d", a=1).broadcast_to([P, D])).then_inc(gb_loaded, 16)
            for c in range(2, NC):
                sp.dma_start(x[:, TC * c:TC * c + TC, :], rows(x_in, c)).then_inc(x_loaded[0][c], 16)
            for m, w in enumerate((wqT, wkT, wvT)):
                sp.dma_start(raw_w[:, m], w.rearrange("(c p) n -> p c n", p=P)).then_inc(wp_loaded, 16)
            sp.dma_start(wo[:], woT.rearrange("(c p) n -> p c n", p=P)).then_inc(wo_loaded, 16)
            sp.wait_ge(w_hi, 4)
            sp.wait_ge(w_lo, 4)
            sp.dma_start(wall_d, wall[:].bitcast(F32)).then_inc(wall_stored, 16)
            for c in range(NC):
                sp.wait_ge(x_done, TC * (c + 1))
                sp.dma_start(rows(x1_d, c), x[:, TC * c:TC * c + TC, :]).then_inc(x1_stored[c], 16)
            sp.wait_ge(wall_stored, 16)
            sp.wait_ge(y_summed, FT)
            for c in range(NC):
                sp.wait_ge(x1_stored[c], 16)
            sp.wait_ge(ones_ready, 1)
            sp.dma_start(K[PARTS:PARTS + NSH].rearrange("r h (a s) -> r (h a) s", s=CH), ones[:].rearrange("r (a s) -> r a s", a=1).broadcast_to([NSH, H * NC, CH])).then_inc(ones_loaded, 16)

            def stack(c):
                for k in range(NB):
                    sp.wait_ge(parts_stored[k], 16 * (c + 1))
                if c == 2:
                    sp.wait_ge(turned, 2 * NC)
                for m, dst in ((0, Q[:, c]), (1, K[:, :, c * CH:(c + 1) * CH])):
                    row = 0
                    for part in range(3):
                        src = part_d[m, :, :, c * CH:(c + 1) * CH]
                        if m == 0:
                            src = src[part:part + 1].broadcast_to([3 - part, D, CH])
                        else:
                            src = src[0:3 - part].rearrange("a (d h) s -> (a d) h s", d=DH)
                        sp.dma_start(dst[row:row + (3 - part) * DH], src).then_inc(qk_loaded[c], 16)
                        row += (3 - part) * DH

            for c in range(NC):
                for w in range(4):
                    n = 4 * c + w
                    m, hc = w // 2, w % 2
                    sp.wait_ge(part_l, n + 1)
                    sp.dma_start(part_d[m, :, hc * P:(hc + 1) * P, c * CH:(c + 1) * CH].rearrange("a d s -> d a s"),
                                 parts[:, n % NB]).then_inc(parts_stored[n % NB], 16)
                if c == STACK0:
                    stack(0)
            stack(1)
            for k in range(2):
                sp.wait_ge(m_loaded[k], 16 * NSH)
                stack(2 + k)
            for u, (c, g) in enumerate(UNITS):
                if u == 0:
                    sp.wait_ge(vj_done, NT)
                    sp.dma_start(x1t[:], rows(x1_d, 0)).then_inc(x1t_loaded, 16)
                sp.wait_ge(acc_out, u + 1)
                sp.dma_start(sums_d[u].rearrange("j r q -> (j r) q"), sums[:, u % 2]).then_inc(sums_stored, 16)
                sp.wait_ge(sums_stored, 16 * (u + 1))
                if g == 0 and c:
                    sp.wait_ge(slot_full, PROJECTED[c - 1])
                sp.dma_start(att[64 * (g % 2):64 * (g % 2) + 64, g // 2, :], sums_d[u, :, 0:DH, :]).then_inc(att_loaded[g], 16)
                if u >= 2:
                    sp.wait_ge(inv_ready, u - 1)
                sp.dma_start(den[:, u % 2], sums_d[u, :, DH, :].rearrange("j (p q) -> j p q", q=G * CH // P)).then_inc(den_loaded, 16)
                if u == NU - 1:
                    sp.wait_ge(qk_done, G * len(STEPS))
                    for k in (1, 2):
                        sp.wait_ge(x2_stored[k], 16)
                        sp.dma_start(x[:, TC * k:TC * k + TC, :], rows(x2_d, k)).then_inc(x_loaded[1][k], 16)
                    sp.dma_start(x[:, TC * (NC - 1):NT, :], rows(x1_d, NC - 1)).then_inc(x_loaded[1][NC - 1], 16)
                sp.wait_ge(inv_ready, u + 1)
                sp.dma_start(inv_d[u].rearrange("(p q) -> p q", p=P), inv[:, u % 2]).then_inc(inv_stored, 16)
                sp.wait_ge(inv_stored, 16 * (u + 1))
                sp.dma_start(rb[64 * (g % 2):64 * (g % 2) + 64, g // 2], inv_d[u].rearrange("(j a q) -> j a q", j=G, a=1).broadcast_to([G, DH, CH])).then_inc(rb_loaded[g], 16)
                if g == 0 and c:
                    sp.wait_ge(slot_free, PROJECTED[c - 1])
                    sp.dma_start(rows(x2_d, c - 1), x1t[:]).then_inc(x2_stored[c - 1], 16)
                    sp.wait_ge(x2_stored[c - 1], 16)
                    if c < NC - 1:
                        sp.dma_start(x1t[:], rows(x1_d, c)).then_inc(x1t_loaded, 16)
                if u == NU - NG:
                    sp.wait_ge(qk_done, G * FIRST[NU - NG])
                    sp.dma_start(x[:, 0:TC, :], rows(x2_d, 0)).then_inc(x_loaded[1][0], 16)
                    sp.dma_start(wall[:].bitcast(F32), wall_d).then_inc(wall_back, 16)
            for c in range(NC - 1):
                sp.wait_ge(x_done, FT + TC * (c + 1))
                sp.dma_start(rows(out, c), x[:, TC * c:TC * c + TC, :]).then_inc(out_stored, 16)
            for k in (0, 2):
                t = NT - TC + k
                sp.wait_ge(x_done, FT + t + 2)
                sp.dma_start(rows(out, NC - 1)[:, k:k + 2], x[:, t:t + 2, :]).then_inc(out_stored, 16)
            sp.wait_ge(out_stored, 16 * (NC + 1))

        @block.gpsimd
        def _(gp):
            count = [0]

            def link(ins):
                count[0] += 1
                ins.then_inc(pool, 1)
                gp.wait_ge(pool, count[0])

            nc.gpsimd.memset(ident[:], 0.0).then_inc(consts_ready, 1)
            nc.gpsimd.memset(mask[:], 0.0).then_inc(consts_ready, 1)
            gp.wait_ge(consts_ready, 2)
            nc.gpsimd.affine_select(out=ident[:], in_=ident[:], compare_op=ALU.not_equal, fill=1.0, base=0,
                                    pattern=[[-1, P]], channel_multiplier=1).then_inc(consts_ready, 1)
            nc.gpsimd.affine_select(out=mask[:, CH - P:CH], in_=mask[:, CH - P:CH], compare_op=ALU.is_ge, fill=LOWEST, base=0,
                                    pattern=[[-1, P]], channel_multiplier=1).then_inc(consts_ready, 1)

            def normalise(u):
                for w in (u - 1, u):
                    gp.wait_ge(rb_loaded[w % NG], 16 * (w // NG + 1))
                    gp.wait_ge(att_loaded[w % NG], 16 * (w // NG + 1))
                k = UNITS[u][1] // 2
                nc.gpsimd.tensor_tensor(att[:, k], att[:, k], rb[:, k], ALU.mult).then_inc(norm_done, 1)

            def add_output(v):
                gp.wait_ge(yh_ready, v + 1)
                link(nc.gpsimd.tensor_tensor(yh[:, v % 2], yh[:, v % 2], gam[:], ALU.mult))
                xt = x[:, v % NT]
                nc.gpsimd.tensor_tensor(xt, xt, yh[:, v % 2], ALU.add).then_inc(x_done, 1)

            def ffn(f):
                for c in range(NC):
                    n = NF * f + c
                    for i in range(IC):
                        u = IC * n + i
                        gp.wait_ge(relu_done, u + 1)
                        if u >= 2:
                            gp.wait_ge(lo_done, u - 1)
                        nc.gpsimd.tensor_tensor(sq[:, u % 2], relu[:, u % NR], relu[:, u % NR], ALU.mult).then_inc(sq_done, 1)
                    gp.wait_ge(gb_ready, 2)
                    for j in range(TC):
                        xt = x[:, TC * c + j]
                        nc.gpsimd.tensor_tensor(xt, xt, bet[:], ALU.add).then_inc(x_beta, 1)
                        if j:
                            add_output(TC * n + j - 1)
                    if n == NC:
                        normalise(NU - 1)

            ffn(0)
            gp.wait_ge(y_done, FT)
            gp.wait_ge(w_lo, 4)
            gp.wait_ge(w_hi, 4)
            nc.gpsimd.memset(V[:, :, :, DH:DH + 1], 1.0).then_inc(v_ones, 1)
            for n in range(4 * NC):
                gp.wait_ge(part_m, n + 1)
                nc.gpsimd.tensor_tensor(parts[:, n % NB, 2], rest[:, n % NRE], parts[:, n % NB, 1], ALU.subtract).then_inc(part_l, 1)

            def clear_diagonal(s):
                u, kt = STEPS[s]
                c = UNITS[u][0]
                if kt >= TC * c:
                    q0 = P * (kt - TC * c)
                    gp.wait_ge(exp_done, G * (s + 1))
                    blk = pr[:, s % 3, :, q0:q0 + P]
                    nc.gpsimd.affine_select(out=blk, in_=blk, compare_op=ALU.is_ge, fill=0.0, base=0,
                                            pattern=[[0, G], [1, P]], channel_multiplier=-1).then_inc(sel_done, 1)

            for event in PLAN:
                kind, what = event
                if kind == "turn":
                    b = what % 2
                    gp.wait_ge(slot_free, SLOT[event] + 1)
                    if what >= 2:
                        gp.wait_ge(m_loaded[b], 16 * NSH * (what // 2))
                    link(nc.gpsimd.tensor_copy(mrow[:, b, 0], neg[:, b]))
                    link(nc.gpsimd.tensor_tensor(mrest[:, b], neg[:, b], mrow[:, b, 0], ALU.subtract))
                    link(nc.gpsimd.tensor_copy(mrow[:, b, 1], mrest[:, b]))
                    nc.gpsimd.tensor_tensor(mrow[:, b, 2], mrest[:, b], mrow[:, b, 1], ALU.subtract).then_inc(mrow_ready, 1)
                elif kind == "exp" and what[1] == SEL_AT and what[0]:
                    clear_diagonal(what[0] - 1)
                elif kind == "norm" and what < NU - 1:
                    normalise(what)
            clear_diagonal(len(STEPS) - 1)
            ffn(1)

        @block.scalar
        def _(act):
            def weight_hi(dst, src, loaded, n):
                act.wait_ge(loaded, n)
                nc.scalar.copy(dst, src).then_inc(w_hi, 1)

            def sqrt_of(c_no):
                act.wait_ge(mv_ready, c_no + 1)
                nc.scalar.activation(sd[:], mv[:, :, 1], ACT.Sqrt, bias=eps_t[:, 0:1]).then_inc(sd_ready, 1)

            def turned_hi(c_no, dst):
                act.wait_ge(turned, c_no + 1)
                nc.scalar.copy(dst, ps[:, 0:KC, :]).then_inc(xT_hi, 1)

            def turn_dst(t, part):
                return (xqT if NC <= t < 2 * NC else xT)[t % 2][part][:]

            def ffn(f):
                if not f:
                    sqrt_of(0)
                    weight_hi(wu[0][:, :, 0:IH], raw_u[:, :, 0:IH], wu_loaded, 16)
                    turned_hi(0, turn_dst(0, 0))
                    weight_hi(wu[0][:, :, IH:I], raw_u[:, :, IH:I], wu2_loaded, 16)

                def sqrt_of_tile(v):
                    act.wait_ge(mv2_ready, v + 1)
                    nc.scalar.activation(sd2[:, v % 2:v % 2 + 1], mv2[:, v % 2, 1:2], ACT.Sqrt, bias=eps_t[:, 0:1]).then_inc(sd2_ready, 1)

                def square(u):
                    act.wait_ge(relu_done, u + 1)
                    if u >= IC and u % IC == 0:
                        act.wait_ge(y_done, TC * (u // IC))
                    nc.scalar.activation(hT[0][:, u % IC], relu[:, u % NR], ACT.Square).then_inc(hi_done, 1)

                for c in range(NC):
                    n = NF * f + c
                    t = 2 * NC * f + c
                    following = t + 1 < 3 * NC
                    for i in range(IC):
                        u = IC * n + i
                        if n == 0 and i == 4:
                            weight_hi(wg[0], raw_g[:], wg_loaded, 32)
                            weight_hi(wd[0], raw_d[:], wd_loaded, 16)
                        if n == 1 and i == 4:
                            for m in range(3):
                                weight_hi(wp[m][0][:], raw_w[:, m], wp_loaded, 48)
                        act.wait_ge(up_done, u + 1)
                        if u >= NR:
                            act.wait_ge(sq_done, u - NR + 1)
                            act.wait_ge(hi_done, u - NR + 1)
                        nc.scalar.activation(relu[:, u % NR], ps[:, 2 + u % 2, :], ACT.Relu).then_inc(relu_done, 1)
                        if i:
                            square(u - 1)
                        if i == 0 and c:
                            sqrt_of_tile(TC * n - 1)
                    square(u)
                    for j in range(TC):
                        v = TC * n + j
                        act.wait_ge(route_ready, v + 1)
                        if v >= 2:
                            act.wait_ge(y_summed, v - 1)
                        nc.scalar.mul(moe[:, v % 2], ps[:, 6 + v % 2, 0:D], route[:, v % 2:v % 2 + 1]).then_inc(moe_scaled, 1)
                        if j == 0 and following:
                            sqrt_of(t + 1)
                        if j == TURN_AFTER + 1 and following:
                            if n >= 1:
                                act.wait_ge(y_done, TC * n)
                            turned_hi(t + 1, turn_dst(t + 1, 0))
                        if j:
                            sqrt_of_tile(v - 1)
                sqrt_of_tile(TC * (n + 1) - 1)

            act.wait_ge(eps_ready, 1)
            nc.scalar.activation(scratch[:], eps_t[:], ACT.Sqrt).then_inc(act_own, 1)
            ffn(0)
            sqrt_of(NC + 1)
            for c in range(NC):
                following = c + 1 < NC

                def middle_part(n):
                    act.wait_ge(rest_done, n + 1)
                    nc.scalar.copy(parts[:, n % NB, 1], rest[:, n % NRE]).then_inc(part_m, 1)

                for w in range(4):
                    n = 4 * c + w
                    act.wait_ge(pj_done, n + 1)
                    if n >= NB:
                        act.wait_ge(parts_stored[n % NB], 16 * (n // NB))
                    nc.scalar.copy(parts[:, n % NB, 0], ps[:, PJ[n % 4], :]).then_inc(part_h, 1)
                    if w == 3 and following:
                        if c:
                            act.wait_ge(vj_done, TC * c)
                        turned_hi(NC + c + 1, turn_dst(NC + c + 1, 0))
                    if w:
                        middle_part(n - 1)
                for j in range(TC):
                    t = TC * c + j
                    act.wait_ge(vj_done, t + 1)
                    if t == 0:
                        act.wait_ge(v_ones, 1)
                    nc.scalar.copy(V[:, t, :, 0:DH], ps[:, 4 + t % 2, 0:D].rearrange("p (h d) -> p h d", h=H)).then_inc(v_done, 1)
                    if j == 0:
                        middle_part(n)
                    if j == 2 and c + 2 < NC:
                        sqrt_of(NC + c + 2)
            for k in range(NB):
                act.wait_ge(parts_stored[k], 16 * NC)
            act.wait_ge(vj_done, NT)
            act.wait_ge(act_own, 1)
            nc.scalar.activation(scratch[:], eps_t[:], ACT.Exp)
            for kind, what in PLAN:
                if kind == "exp":
                    s, j = what
                    e = G * s + j
                    u, kt = STEPS[s]
                    c = UNITS[u][0]
                    q0 = max(0, P * (kt - TC * c))
                    act.wait_ge(qk_done, e + 1)
                    if s >= 3 and j == 0:
                        act.wait_ge(pv_done, s - 2)
                    nc.scalar.activation(pr[:, s % 3, j, q0:CH], ps[:, e % 3, q0:CH], ACT.Exp, scale=SCALE).then_inc(exp_done, 1)
                elif kind == "norm_x":
                    sqrt_of(2 * NC)
                elif kind == "turn_x":
                    act.wait_ge(qk_done, G * len(STEPS))
                    act.wait_ge(slot_full, SLOTS)
                    turned_hi(2 * NC, turn_dst(2 * NC, 0))
                elif kind == "acc":
                    c, g = UNITS[what]
                    act.wait_ge(pv_done, FIRST[what + 1])
                    if what >= 2:
                        act.wait_ge(sums_stored, 16 * (what - 1))
                    nc.scalar.copy(sums[:, what % 2], ps[:, 3, :]).then_inc(acc_out, 1)
                elif kind == "rows":
                    c, g = UNITS[what]
                    act.wait_ge(mrow_ready, what + 1)
                    for a in range(NSH):
                        act.dma_start(Q[PARTS + a:PARTS + a + 1, c, G * g:G * g + G, :].rearrange("o j (i q) -> o (j i) q", q=P),
                                      mrow[:, what % 2, a, :]).then_inc(m_loaded[what % 2], 16)
            ffn(1)

        @block.vector
        def _(v_):
            count = [0]

            def link(ins):
                count[0] += 1
                ins.then_inc(dve, 1)
                v_.wait_ge(dve, count[0])

            def weight_lo(dst, src, hi, n):
                v_.wait_ge(w_hi, n)
                nc.vector.tensor_tensor(dst, src, hi.bitcast(F32), ALU.subtract).then_inc(w_lo, 1)

            def ln_stats(t, j):
                c = t % NC
                if j == 0:
                    if NC <= t < 2 * NC:
                        v_.wait_ge(x_done, TC * (c + 1))
                    elif t:
                        v_.wait_ge(x_loaded[t // (2 * NC)][c], 16)
                    if t == 3 * NC - 1:
                        v_.wait_ge(slot_free, SLOTS + TC)
                if t == 0:
                    v_.wait_ge(tile_loaded[j], 16)
                nc.vector.bn_stats(stat[:, j], x[:, TC * c + j]).then_inc(stats_done, 1)

            def ln_mean(t):
                v_.wait_ge(stats_done, TC * (t + 1))
                for j in range(TC):
                    last = nc.vector.bn_aggr(mv[:, j], stat[:, j])
                last.then_inc(mv_ready, 1)

            def ln_rows(t):
                v_.wait_ge(sd_ready, t + 1)
                link(nc.vector.reciprocal(rs[:], sd[:]))
                if t >= 2:
                    v_.wait_ge(turned, t - 1)
                for j in range(TC):
                    last = nc.vector.tensor_scalar(xn[:, t % 2, j], x[:, TC * (t % NC) + j], mv[:, j, 0:1], rs[:, j:j + 1],
                                                   ALU.subtract, ALU.mult)
                last.then_inc(xn_ready, 1)

            def layer_norm(t):
                for j in range(TC):
                    ln_stats(t, j)
                ln_mean(t)
                ln_rows(t)

            def turn_dst(t, part):
                return (xqT if NC <= t < 2 * NC else xT)[t % 2][part][:]

            def turned_lo(t):
                v_.wait_ge(xT_hi, t + 1)
                nc.vector.tensor_tensor(turn_dst(t, 1), ps[:, 0:KC, :], turn_dst(t, 0).bitcast(F32), ALU.subtract).then_inc(xT_lo, 1)

            def halve_gamma_beta():
                v_.wait_ge(gb_loaded, 32)
                nc.vector.tensor_scalar(gam[:], gam[:], 0.5, None, ALU.mult).then_inc(gb_ready, 1)
                nc.vector.tensor_scalar(bet[:], bet[:], 0.5, None, ALU.mult).then_inc(gb_ready, 1)

            def ffn(f):
                first = 2 * NC * f
                if not f:
                    layer_norm(0)
                    weight_lo(wu[1][:, :, 0:IH], raw_u[:, :, 0:IH], wu[0][:, :, 0:IH], 1)
                    turned_lo(first)
                    weight_lo(wu[1][:, :, IH:I], raw_u[:, :, IH:I], wu[0][:, :, IH:I], 2)

                def normalised(v):
                    k = v % 2
                    v_.wait_ge(sd2_ready, v + 1)
                    link(nc.vector.reciprocal(rs2[:, k:k + 1], sd2[:, k:k + 1]))
                    if v >= 2:
                        v_.wait_ge(x_done, v - 1)
                    nc.vector.tensor_scalar(yh[:, k], y[:, k], mv2[:, k, 0:1], rs2[:, k:k + 1], ALU.subtract, ALU.mult).then_inc(yh_ready, 1)
                    if v % TC == TC - 1:
                        v_.wait_ge(yh_ready, v + 1)
                        link(nc.vector.tensor_tensor(yh[:, k], yh[:, k], gam[:], ALU.mult))
                        v_.wait_ge(x_beta, v + 1)
                        nc.vector.tensor_tensor(x[:, v % NT], x[:, v % NT], yh[:, k], ALU.add).then_inc(x_done, 1)

                for c in range(NC):
                    n = NF * f + c
                    t = first + c
                    following = t + 1 < 3 * NC
                    for i in range(IC):
                        u = IC * n + i
                        if n == 0 and i == 4:
                            weight_lo(wg[1], raw_g[:], wg[0], 3)
                            weight_lo(wd[1], raw_d[:], wd[0], 4)
                        if n == 1 and i == 4:
                            for m in range(3):
                                weight_lo(wp[m][1][:], raw_w[:, m], wp[m][0][:], 5 + m)
                        v_.wait_ge(hi_done, u + 1)
                        v_.wait_ge(sq_done, u + 1)
                        nc.vector.tensor_tensor(hT[1][:, i], sq[:, u % 2], hT[0][:, i].bitcast(F32), ALU.subtract).then_inc(lo_done, 1)
                        if i == 0 and c:
                            normalised(TC * n - 1)
                        if n == 0 and i == 3:
                            halve_gamma_beta()
                        if n == NC and i == 2:
                            inverse(NU - 1)
                        if n == NC + 1 and LAST_PROJ <= i < LAST_PROJ + TC:
                            projected(NC - 1, i - LAST_PROJ, SLOTS + i - LAST_PROJ)
                        if following and STATS_AT <= i < STATS_AT + TC:
                            ln_stats(t + 1, i - STATS_AT)
                        if following and i == IC - 1:
                            ln_mean(t + 1)
                    for j in range(TC):
                        v = TC * n + j
                        k = v % 2
                        v_.wait_ge(moe_done, v + 1)
                        link(nc.vector.max(top8[:], ps[:, 6 + k, D:YW]))
                        nc.vector.tensor_tensor(route[:, k:k + 1], top8[:, 0:1], top8[:, 1:2], ALU.add).then_inc(route_ready, 1)
                        if j:
                            normalised(v - 1)
                        if j == 0 and following:
                            ln_rows(t + 1)
                        v_.wait_ge(moe_scaled, v + 1)
                        v_.wait_ge(y_done, v + 1)
                        nc.vector.tensor_tensor(y[:, k], ps[:, 4 + k, 0:D], moe[:, k], ALU.add).then_inc(y_summed, 1)
                        if j == TURN_AFTER + 1 and following:
                            turned_lo(t + 1)
                        v_.wait_ge(y_summed, v + 1)
                        link(nc.vector.bn_stats(stat2[:], y[:, k]))
                        nc.vector.bn_aggr(mv2[:, k], stat2[:]).then_inc(mv2_ready, 1)
                normalised(TC * (n + 1) - 1)

            def inverse(u):
                v_.wait_ge(den_loaded, 16 * (u + 1))
                if u >= 2:
                    v_.wait_ge(inv_stored, 16 * (u - 1))
                nc.vector.reciprocal(inv[:, u % 2], den[:, u % 2]).then_inc(inv_ready, 1)

            def projected(c, k, z):
                v_.wait_ge(slot_full, z + 1)
                if c < NC - 1:
                    v_.wait_ge(x1t_loaded, 16 * (c + 1))
                    xt = x1t[:, k, :]
                else:
                    v_.wait_ge(x_loaded[1][c], 16)
                    xt = x[:, TC * c + k, :]
                nc.vector.tensor_tensor(xt, ps[:, bank_of(z), 0:D], xt, ALU.add).then_inc(slot_free, 1)

            def max_of_piece(what):
                z = SLOT[("max", what)]
                slot = ps[:, bank_of(z), :]
                u, i, ch, j = PIECES[what]
                c = UNITS[u][0]
                mx = mxp[:, u % 3]
                v_.wait_ge(slot_full, z + 1)
                if (i, ch, j) == (0, 0, 0) and u >= 3:
                    v_.wait_ge(top_ready, u - 2)
                if ch < c:
                    last = nc.vector.tensor_reduce(mx[:, ch, j, i:i + 1], slot[:, 0:CH], AX.X, ALU.max)
                else:
                    w = P * (i + 1)
                    last = nc.vector.tensor_tensor_reduce(slot[:, 0:w], slot[:, 0:w], mask[:, CH - w:CH], 1.0, LOWEST,
                                                          ALU.add, ALU.max, mx[:, c, j, i:i + 1])
                last.then_inc(slot_free, 1)

            def maxima(event):
                kind, what = event
                if kind == "max":
                    max_of_piece(what)
                elif kind == "top":
                    c = UNITS[what][0]
                    v_.wait_ge(slot_free, SLOT[("max", LAST_PIECE[what])] + 1)
                    nc.vector.tensor_reduce(mcol[:, what % 2], mxp[:, what % 3, 0:c + 1].rearrange("p s j i -> p (j i) s"), AX.X,
                                            ALU.max).then_inc(top_ready, 1)
                elif kind == "turn":
                    z = SLOT[event]
                    v_.wait_ge(slot_full, z + 1)
                    if what >= 2:
                        v_.wait_ge(mrow_ready, what - 1)
                    nc.vector.tensor_scalar(neg[:, what % 2], ps[0:G * TC, bank_of(z), 0:P], -1.0, None, ALU.mult).then_inc(slot_free, 1)

            def early(n):
                for event in EARLY_EVENTS[n]:
                    if event[0] in ("max", "top", "turn"):
                        maxima(event)

            nc.vector.memset(eps_t[:], EPS).then_inc(eps_ready, 1)
            nc.vector.memset(ones[:], 1.0).then_inc(ones_ready, 1)
            ffn(0)
            layer_norm(NC + 1)
            for c in range(NC):
                t = NC + c
                following = c + 1 < NC
                for w in range(4):
                    n = 4 * c + w
                    v_.wait_ge(part_h, n + 1)
                    if n >= NRE:
                        v_.wait_ge(part_l, n - NRE + 1)
                    nc.vector.tensor_tensor(rest[:, n % NRE], ps[:, PJ[n % 4], :], parts[:, n % NB, 0], ALU.subtract).then_inc(rest_done, 1)
                    if c == NC - 1:
                        early(w)
                if following:
                    turned_lo(t + 1)
                if c + 2 < NC:
                    layer_norm(t + 2)
                if c == NC - 2:
                    v_.wait_ge(consts_ready, 4)
            for n in range(4, len(EARLY_EVENTS)):
                early(n)
            nc.vector.memset(ps[:, 3, :], 0.0).then_inc(acc_zeroed, 1)
            v_.wait_ge(part_l, 4 * NC)
            for event in PLAN[MAIN:]:
                kind, what = event
                if kind in ("max", "top", "turn"):
                    maxima(event)
                elif kind == "inv":
                    if what < NU - 1:
                        inverse(what)
                elif kind == "proj":
                    projected(*what, SLOT[event])
                elif kind == "norm_x":
                    layer_norm(2 * NC)
                elif kind == "turn_x":
                    turned_lo(2 * NC)
            ffn(1)

        @block.tensor
        def _(pe):
            def turn(t):
                src = xn[:, t % 2]
                pe.wait_ge(xn_ready, t + 1)
                if t:
                    pe.wait_ge(xT_hi, t)
                    pe.wait_ge(xT_lo, t)
                for j in range(TC):
                    for k in range(KC):
                        mm = nc.tensor.transpose(ps[:, k, P * j:P * j + P], src[:, j, P * k:P * k + P], ident[:])
                mm.then_inc(turned, 1)

            def product(dst, lhs, rhs, chunks):
                n = 0
                for k in chunks:
                    for a, b in ((0, 0), (0, 1), (1, 0)):
                        mm = nc.tensor.matmul(dst, lhs(a, k), rhs(b, k), start=(n == 0), stop=(n == 3 * len(chunks) - 1))
                        n += 1
                return mm

            def ffn(f):
                first = 2 * NC * f
                if f:
                    pe.wait_ge(wall_back, 16)
                else:
                    turn(first)
                for c in range(NC):
                    n = NF * f + c
                    xt = xT[c % 2]
                    t = first + c
                    pe.wait_ge(xT_hi, t + 1)
                    pe.wait_ge(xT_lo, t + 1)
                    for i in range(IC):
                        u = IC * n + i
                        if n == 0 and i % 4 == 0:
                            pe.wait_ge(w_hi, 1 + i // 4)
                            pe.wait_ge(w_lo, 1 + i // 4)
                        if n == NC and i == 1:
                            pe.wait_ge(acc_out, NU)
                        if u >= 2:
                            pe.wait_ge(relu_done, u - 1)
                        product(ps[:, 2 + u % 2, :], lambda a, k: wu[a][:, k, P * i:P * i + P], lambda b, k: xt[b][:, k, :],
                                range(KC)).then_inc(up_done, 1)
                        if n == NC + 1 and LAST_PROJ <= i < LAST_PROJ + TC:
                            project(NC - 1, i - LAST_PROJ, SLOTS + i - LAST_PROJ)
                    if n == 0:
                        pe.wait_ge(w_hi, 4)
                        pe.wait_ge(w_lo, 4)
                    if n == NC:
                        pe.wait_ge(slot_free, SLOTS)
                    if n == NC + 1:
                        pe.wait_ge(slot_free, SLOTS + TC)
                    for j in range(TC):
                        v = TC * n + j
                        if v >= 2:
                            pe.wait_ge(moe_scaled, v - 1)
                            pe.wait_ge(y_summed, v - 1)
                            pe.wait_ge(route_ready, v - 1)
                        product(ps[:, 6 + v % 2, 0:YW], lambda a, k: xt[a][:, k, P * j:P * j + P], lambda b, k: wg[b][:, k, :],
                                range(KC)).then_inc(moe_done, 1)
                        for i in range(IC):
                            if j == 0:
                                pe.wait_ge(lo_done, IC * n + i + 1)
                            for m, (a, b) in enumerate(((0, 0), (0, 1), (1, 0))):
                                mm = nc.tensor.matmul(ps[:, 4 + v % 2, 0:D], hT[a][:, i, P * j:P * j + P], wd[b][:, i, :],
                                                      start=(i == 0 and m == 0), stop=(i == IC - 1 and m == 2))
                        mm.then_inc(y_done, 1)
                        if j == TURN_AFTER and t + 1 < 3 * NC:
                            turn(t + 1)

            def project(c, k, z):
                pe.wait_ge(slot_free, z - SLOT_BANKS + 1)
                if c == NC - 1:
                    pe.wait_ge(moe_scaled, TC * (NC + 1))
                    pe.wait_ge(y_summed, TC * (NC + 1))
                    pe.wait_ge(route_ready, TC * (NC + 1))
                pe.wait_ge(norm_done, NG // 2 * (c + 1))
                for h in range(KC):
                    mm = nc.tensor.matmul(ps[:, bank_of(z), 0:D], att[:, h, P * k:P * k + P], wo[:, h, :],
                                          start=(h == 0), stop=(h == KC - 1))
                mm.then_inc(slot_full, 1)

            def slot_is_free(z):
                if 2 <= z < EARLY:
                    pe.wait_ge(slot_free, z - 1)
                elif z >= EARLY + SLOT_BANKS:
                    pe.wait_ge(slot_free, z - SLOT_BANKS + 1)

            def piece(what):
                z = SLOT[("max", what)]
                u, i, ch, j = PIECES[what]
                c, g = UNITS[u]
                slot_is_free(z)
                if (g, i, ch, j) == (0, 0, 0, 0):
                    pe.wait_ge(qk_loaded[c], 16 * 6)
                w = CH if ch < c else P * (i + 1)
                h = G * g + j
                nc.tensor.matmul(ps[:, bank_of(z), 0:w], Q[0:PARTS, c, h, P * i:P * i + P],
                                 K[0:PARTS, h, CH * ch:CH * ch + w], start=True, stop=True).then_inc(slot_full, 1)

            def maxima(event):
                kind, what = event
                if kind == "max":
                    piece(what)
                elif kind == "turn":
                    slot_is_free(SLOT[event])
                    pe.wait_ge(top_ready, what + 1)
                    nc.tensor.transpose(ps[0:G * TC, bank_of(SLOT[event]), 0:P], mcol[:, what % 2], ident[:]).then_inc(slot_full, 1)

            def early(n):
                for event in EARLY_EVENTS[n]:
                    maxima(event)

            pe.wait_ge(consts_ready, 3)
            for n in range(WARM):
                mm = nc.tensor.transpose(ps[:, 7, 0:P], ident[:], ident[:])
            ffn(0)
            pe.wait_ge(w_hi, 7)
            pe.wait_ge(w_lo, 7)
            for c in range(NC):
                t = NC + c
                if c == 0:
                    pe.wait_ge(relu_done, IC * NF)
                    pe.wait_ge(y_summed, FT)
                pe.wait_ge(xT_hi, t + 1)
                pe.wait_ge(xT_lo, t + 1)
                xt = xqT[c % 2]
                for w in range(4):
                    n = 4 * c + w
                    m, hc = w // 2, w % 2
                    if n >= 4:
                        pe.wait_ge(rest_done, n - 3)
                    product(ps[:, PJ[n % 4], :], lambda a, k: wp[m][a][:, k, P * hc:P * hc + P], lambda b, k: xt[b][:, k, :],
                            range(KC)).then_inc(pj_done, 1)
                    if w == TURN_W and c + 1 < NC:
                        turn(NC + c + 1)
                    if c == NC - 1:
                        early(w)
                for j in range(TC):
                    t = TC * c + j
                    if t >= 2:
                        pe.wait_ge(v_done, t - 1)
                    product(ps[:, 4 + t % 2, 0:D], lambda a, k: xt[a][:, k, P * j:P * j + P], lambda b, k: wp[2][b][:, k, :],
                            range(KC)).then_inc(vj_done, 1)
                    if c == NC - 1:
                        early(4 + j)
            pe.wait_ge(v_done, NT)
            pe.wait_ge(rest_done, 4 * NC)
            pe.wait_ge(slot_free, EARLY)
            pe.wait_ge(acc_zeroed, 1)
            pe.wait_ge(ones_loaded, 16)
            pe.wait_ge(wo_loaded, 16)
            for event in PLAN[MAIN:]:
                kind, what = event
                if kind in ("max", "turn"):
                    maxima(event)
                elif kind == "exp":
                    s, j = what
                    e = G * s + j
                    u, kt = STEPS[s]
                    c, g = UNITS[u]
                    if e >= 3:
                        pe.wait_ge(exp_done, e - 2)
                    if kt == 0 and j == 0:
                        pe.wait_ge(m_loaded[u % 2], 16 * NSH * (u // 2 + 1))
                    q0 = max(0, P * (kt - TC * c))
                    h = G * g + j
                    nc.tensor.matmul(ps[:, e % 3, q0:CH], K[0:PARTS + NSH, h, P * kt:P * kt + P], Q[0:PARTS + NSH, c, h, q0:CH],
                                     start=True, stop=True).then_inc(qk_done, 1)
                elif kind == "pv":
                    s = what
                    u, kt = STEPS[s]
                    c, g = UNITS[u]
                    q0 = max(0, P * (kt - TC * c))
                    pe.wait_ge(exp_done, G * (s + 1))
                    if kt >= TC * c:
                        pe.wait_ge(sel_done, DIAG[s + 1])
                    if kt == 0 and u:
                        pe.wait_ge(acc_out, u)
                    for j in range(G):
                        mm = nc.tensor.matmul(ps[32 * j:32 * j + DH + 1, 3, q0:CH], V[:, kt, G * g + j, :], pr[:, s % 3, j, q0:CH],
                                              start=(kt == 0), stop=(kt == TC * c + TC - 1))
                    mm.then_inc(pv_done, 1)
                elif kind == "proj":
                    project(*what, SLOT[event])
                elif kind == "turn_x":
                    pe.wait_ge(exp_done, G * len(STEPS))
                    turn(2 * NC)
            ffn(1)


def kernel(L0_attn_x, L0_attn_Wq, L0_attn_Wk, L0_attn_Wv, L0_attn_Wo, L0_ffn_gate_w, L0_ffn_up_w, L0_ffn_down_w,
           L0_ffn_expert_weight, L0_ffn_ln_gamma, L0_ffn_ln_beta):
    import numpy as np
    import concourse.bacc as bacc
    from concourse.bass_utils import run_bass_kernel_spmd

    def by_width(w):
        return np.ascontiguousarray(w.reshape(D, H, DH).transpose(0, 2, 1).reshape(D, D))

    arrays = {
        "x": np.asarray(L0_attn_x).reshape(S, D),
        "wqT": by_width(np.asarray(L0_attn_Wq).T),
        "wkT": by_width(np.asarray(L0_attn_Wk).T),
        "wvT": np.ascontiguousarray(np.asarray(L0_attn_Wv).T),
        "woT": np.ascontiguousarray(np.asarray(L0_attn_Wo).T),
        "gate_w": np.ascontiguousarray(L0_ffn_gate_w),
        "up_w": np.ascontiguousarray(L0_ffn_up_w),
        "down_w": np.ascontiguousarray(L0_ffn_down_w),
        "expert_w": np.ascontiguousarray(L0_ffn_expert_weight),
        "gamma": np.ascontiguousarray(L0_ffn_ln_gamma),
        "beta": np.ascontiguousarray(L0_ffn_ln_beta),
    }
    nc = bacc.Bacc("TRN2", target_bir_lowering=False, num_devices=1)
    args = [nc.dram_tensor(f"in_{n}", a.shape, mybir.dt.from_np(a.dtype), kind="ExternalInput").ap() for n, a in arrays.items()]
    res = nc.dram_tensor("res", (S, D), F32, kind="ExternalOutput").ap()
    build(nc, *args, res)
    r = run_bass_kernel_spmd(nc, [{f"in_{n}": a for n, a in arrays.items()}], core_ids=[0])
    return r.results[0]["res"].reshape(1, S, D)
```
